# Optimizing a Trainium2 kernel written in Bass

```python
import numpy as np
import jax
import jax.numpy as jnp

def _softmax(x, axis=-1):
    return jax.nn.softmax(x, axis=axis)

def _gelu(x):
    return jax.nn.gelu(x, approximate=True)

def _silu(x):
    return jax.nn.silu(x)

def _sigmoid(x):
    return jax.nn.sigmoid(x)

def _layernorm(x, axis=-1, eps=1e-05):
    m = jnp.mean(x, axis=axis, keepdims=True)
    v = jnp.var(x, axis=axis, keepdims=True)
    return (x - m) / jnp.sqrt(v + eps)

def _scatter_add(tgt, idx, src, axis=0):
    return tgt.at[idx].add(src)

def _segment_sum(src, seg, n):
    return jax.ops.segment_sum(src, seg, n)
kernel_name = 'mk_seq_postln_d1_jaxref_r8_45a0e1'

def setup_inputs(seed: int=0):
    np.random.seed(seed)
    _w = jnp.asarray

    def _L0_attn_setup():
        import jax, jax.numpy as jnp
        import numpy as np
        DIM = 128
        NUM_HEADS = 16
        HEAD_DIM = DIM // NUM_HEADS
        EPS = 1e-06

        def _apply_rope(q, k):
            B, N, H, D = q.shape
            half = D // 2
            freqs = 1.0 / 1250 ** (jnp.arange(0, half, dtype=jnp.float32) / half)
            t = jnp.arange(N, dtype=jnp.float32)
            freqs = jnp.outer(t, freqs)
            emb = jnp.concatenate([freqs, freqs], axis=-1)
            cos = jnp.cos(emb)[None, :, None, :]
            sin = jnp.sin(emb)[None, :, None, :]

            def rot(x):
                x1, x2 = (x[..., :half], x[..., half:])
                return jnp.concatenate([-x2, x1], axis=-1)
            return (q * cos + rot(q) * sin, k * cos + rot(k) * sin)

        def _rmsnorm(x, scale):
            var = jnp.mean(jnp.square(x.astype(jnp.float32)), axis=-1, keepdims=True)
            return (x * jax.lax.rsqrt(var + EPS) * scale).astype(x.dtype)
        key = jax.random.key(seed)
        ks = jax.random.split(key, 6)
        B, N = (4, 256)
        x = jax.random.normal(ks[0], (B, N, DIM), dtype=jnp.float32)
        lim_qkv = float(np.sqrt(6.0 / (DIM + 3 * DIM)))
        w_qkv = jax.random.uniform(ks[1], (DIM, 3 * DIM), jnp.float32, -lim_qkv, lim_qkv)
        q_scale = jnp.ones((HEAD_DIM,), jnp.float32)
        k_scale = jnp.ones((HEAD_DIM,), jnp.float32)
        lim_p = float(np.sqrt(6.0 / (DIM + DIM)))
        w_proj = jax.random.uniform(ks[2], (DIM, DIM), jnp.float32, -lim_p, lim_p)
        b_proj = jnp.zeros((DIM,), jnp.float32)
        return {'x': x, 'w_qkv': w_qkv, 'q_scale': q_scale, 'k_scale': k_scale, 'w_proj': w_proj, 'b_proj': b_proj}
    _L0_attn_in = _L0_attn_setup()

    def _L0_ffn_setup():
        import jax, jax.numpy as jnp
        import numpy as np
        D_IN, D_HID = (128, 512)

        def _ternary(key, shape):
            return jax.random.randint(key, shape, -1, 2).astype(jnp.float32)

        def _tlin(x, w, s):
            return jnp.einsum('bsi,oi->bso', x, w) * s
        key = jax.random.key(seed)
        ks = jax.random.split(key, 12)
        inv = lambda fan: 1.0 / np.sqrt(fan).astype(np.float32)
        return {'x': jax.random.normal(ks[0], (4, 256, D_IN), dtype=jnp.float32), 'w1_w': _ternary(ks[1], (D_HID, D_IN)), 'w1_s': jax.random.uniform(ks[2], (D_HID,), dtype=jnp.float32) * inv(D_IN), 'w2_w': _ternary(ks[3], (D_HID, D_IN)), 'w2_s': jax.random.uniform(ks[4], (D_HID,), dtype=jnp.float32) * inv(D_IN), 'h1_w': _ternary(ks[5], (D_HID, D_HID)), 'h1_s': jax.random.uniform(ks[6], (D_HID,), dtype=jnp.float32) * inv(D_HID), 'h2_w': _ternary(ks[7], (D_HID, D_HID)), 'h2_s': jax.random.uniform(ks[8], (D_HID,), dtype=jnp.float32) * inv(D_HID), 'w3_w': _ternary(ks[9], (D_IN, D_HID)), 'w3_s': jax.random.uniform(ks[10], (D_IN,), dtype=jnp.float32) * inv(D_HID)}
    _L0_ffn_in = _L0_ffn_setup()
    _d = {'L0_attn_x': _L0_attn_in['x'], 'L0_attn_w_qkv': _L0_attn_in['w_qkv'], 'L0_attn_q_scale': _L0_attn_in['q_scale'], 'L0_attn_k_scale': _L0_attn_in['k_scale'], 'L0_attn_w_proj': _L0_attn_in['w_proj'], 'L0_attn_b_proj': _L0_attn_in['b_proj'], 'L0_ffn_w1_w': _L0_ffn_in['w1_w'], 'L0_ffn_w1_s': _L0_ffn_in['w1_s'], 'L0_ffn_w2_w': _L0_ffn_in['w2_w'], 'L0_ffn_w2_s': _L0_ffn_in['w2_s'], 'L0_ffn_h1_w': _L0_ffn_in['h1_w'], 'L0_ffn_h1_s': _L0_ffn_in['h1_s'], 'L0_ffn_h2_w': _L0_ffn_in['h2_w'], 'L0_ffn_h2_s': _L0_ffn_in['h2_s'], 'L0_ffn_w3_w': _L0_ffn_in['w3_w'], 'L0_ffn_w3_s': _L0_ffn_in['w3_s']}
    _x0 = _d['L0_attn_x']
    _d['L0_attn_x'] = jax.random.normal(jax.random.fold_in(jax.random.key(seed), 1), (2, 1024, 128), dtype=_x0.dtype)
    del _x0
    return _d

def reference(L0_attn_x, L0_attn_w_qkv, L0_attn_q_scale, L0_attn_k_scale, L0_attn_w_proj, L0_attn_b_proj, L0_ffn_w1_w, L0_ffn_w1_s, L0_ffn_w2_w, L0_ffn_w2_s, L0_ffn_h1_w, L0_ffn_h1_s, L0_ffn_h2_w, L0_ffn_h2_s, L0_ffn_w3_w, L0_ffn_w3_s):

    def _L0_attn_ref(x, w_qkv, q_scale, k_scale, w_proj, b_proj):
        import jax, jax.numpy as jnp
        import numpy as np
        DIM = 128
        NUM_HEADS = 16
        HEAD_DIM = DIM // NUM_HEADS
        EPS = 1e-06

        def _apply_rope(q, k):
            B, N, H, D = q.shape
            half = D // 2
            freqs = 1.0 / 1250 ** (jnp.arange(0, half, dtype=jnp.float32) / half)
            t = jnp.arange(N, dtype=jnp.float32)
            freqs = jnp.outer(t, freqs)
            emb = jnp.concatenate([freqs, freqs], axis=-1)
            cos = jnp.cos(emb)[None, :, None, :]
            sin = jnp.sin(emb)[None, :, None, :]

            def rot(x):
                x1, x2 = (x[..., :half], x[..., half:])
                return jnp.concatenate([-x2, x1], axis=-1)
            return (q * cos + rot(q) * sin, k * cos + rot(k) * sin)

        def _rmsnorm(x, scale):
            var = jnp.mean(jnp.square(x.astype(jnp.float32)), axis=-1, keepdims=True)
            return (x * jax.lax.rsqrt(var + EPS) * scale).astype(x.dtype)
        B, N, C = x.shape
        qkv = jnp.einsum('bnc,cd->bnd', x, w_qkv).reshape(B, N, 3, NUM_HEADS, HEAD_DIM)
        q, k, v = (qkv[:, :, 0], qkv[:, :, 1], qkv[:, :, 2])
        q = _rmsnorm(q, q_scale)
        k = _rmsnorm(k, k_scale)
        q, k = _apply_rope(q, k)
        q = q.astype(jnp.float32) * HEAD_DIM ** (-0.5)
        k = k.astype(jnp.float32)
        v = v.astype(jnp.float32)
        logits = jnp.einsum('bqhd,bkhd->bhqk', q, k)
        attn = jax.nn.softmax(logits, axis=-1)
        out = jnp.einsum('bhqk,bkhd->bqhd', attn, v).reshape(B, N, C)
        return jnp.einsum('bnc,cd->bnd', out, w_proj) + b_proj

    def _L0_ffn_ref(x, w1_w, w1_s, w2_w, w2_s, h1_w, h1_s, h2_w, h2_s, w3_w, w3_s):
        import jax, jax.numpy as jnp
        import numpy as np
        D_IN, D_HID = (128, 512)

        def _ternary(key, shape):
            return jax.random.randint(key, shape, -1, 2).astype(jnp.float32)

        def _tlin(x, w, s):
            return jnp.einsum('bsi,oi->bso', x, w) * s
        h = jax.nn.silu(_tlin(x, w1_w, w1_s)) * _tlin(x, w2_w, w2_s)
        h = jax.nn.gelu(_tlin(h, h1_w, h1_s), approximate=False)
        h = jax.nn.gelu(_tlin(h, h2_w, h2_s), approximate=False)
        return _tlin(h, w3_w, w3_s)
    x = L0_attn_x
    x = _layernorm(x + _L0_attn_ref(x, L0_attn_w_qkv, L0_attn_q_scale, L0_attn_k_scale, L0_attn_w_proj, L0_attn_b_proj), axis=-1)
    x = _layernorm(x + _L0_ffn_ref(x, L0_ffn_w1_w, L0_ffn_w1_s, L0_ffn_w2_w, L0_ffn_w2_s, L0_ffn_h1_w, L0_ffn_h1_s, L0_ffn_h2_w, L0_ffn_h2_s, L0_ffn_w3_w, L0_ffn_w3_s), axis=-1)
    return x

_drawn_inputs = setup_inputs


def setup_inputs(seed=0):
    import zlib

    import numpy as np

    out = dict(_drawn_inputs(seed))
    spreads = {'L0_attn_q_scale': (1.0, 0.6), 'L0_attn_k_scale': (1.0, 0.6), 'L0_attn_b_proj': (0.0, 0.1)}
    factors = {'L0_ffn_w1_w': 8.0,
     'L0_ffn_w1_s': 8.0,
     'L0_ffn_w2_w': 8.0,
     'L0_ffn_w2_s': 8.0,
     'L0_ffn_h1_w': 8.0,
     'L0_ffn_h1_s': 8.0,
     'L0_ffn_h2_w': 8.0,
     'L0_ffn_h2_s': 8.0,
     'L0_ffn_w3_w': 8.0,
     'L0_ffn_w3_s': 8.0}
    for name, (base, spread) in spreads.items():
        noise = np.random.default_rng([zlib.crc32(name.encode()), seed]).standard_normal(out[name].shape)
        drawn = base * np.exp(spread * noise) if base else spread * noise
        out[name] = jnp.asarray(drawn.astype(out[name].dtype))
    for name, factor in factors.items():
        out[name] = (out[name] * factor).astype(out[name].dtype)
    return out
```

```python
from contextlib import ExitStack

import numpy as np

import concourse.bass as bass
from concourse import mybir

F32 = mybir.dt.float32
F32R = mybir.dt.float32r
BF16 = mybir.dt.bfloat16
I32 = mybir.dt.int32
ALU = mybir.AluOpType
ACT = mybir.ActivationFunctionType
AX = mybir.AxisListType

P = 128
BATCH, SEQ, DIM = 2, 1024, 128
HEADS, HD = 16, 8
TOK = BATCH * SEQ
HID = 512
CH = 512
NCH = TOK // CH
TILES = CH // P
HG = 4
NG = HEADS // HG
KT = SEQ // P
STEPS = NG * KT
PARTS = 3
MROW = PARTS * PARTS * HD
KROWS = 96
HM = HID // P
VW = HD + 1
EPS_RMS, EPS_LN = 1e-6, 1e-5
LOGIT_BOUND = 60.0

MIX_FIRST = 4
MIX_CHUNK = 26
CHAIN_CHUNK = 13

C_S1, C_S2, C_H1, C_H2, C_W3 = 0, 4, 8, 12, 16
C_Q, C_QS, C_K, C_KS = 17, 18, 19, 20
NCOL = 21


def wait(eng, sem, count):
    if isinstance(count, int) and count <= 0:
        return
    eng.wait_ge(sem, count)


def build(nc, x_t, x_n, w_qkv, cols, scale_rows, bias, w_proj, w1, w2, h1, h2, w3, cosines, sines, means, eye, out):
    ctx = ExitStack()
    with ctx:
        def sb(name, shape, dt):
            return ctx.enter_context(nc.sbuf_tensor(name, shape, dt))

        def sem(name):
            return ctx.enter_context(nc.semaphore(name))

        q_scr = nc.dram_tensor("q_scr", [HEADS, 5 * HD, TOK], BF16).ap()
        k_scr = nc.dram_tensor("k_scr", [HEADS, 3 * HD, TOK], BF16).ap()
        m_scr = nc.dram_tensor("m_scr", [PARTS, HEADS, TOK], BF16).ap()

        xT = sb("xT", [P, TOK], F32)
        xb = sb("xb", [P, NCH * TILES, P], F32)
        wq = sb("wq", [P, 5 * P], F32)
        col = sb("col", [P, NCOL], F32)
        rope = sb("rope", [P, 4 * CH], F32)
        cosT, sinT = rope[:, 0:SEQ], rope[:, SEQ:2 * SEQ]
        attnT, yT = rope[:, 0:CH], rope[:, CH:2 * CH]
        x1, yo = (rope[:, i * CH:(i + 1) * CH].rearrange("p (t c) -> p t c", t=TILES) for i in (2, 3))
        mean8 = sb("mean8", [P, P], F32)
        ident = sb("ident", [P, P], F32)
        bias_b = sb("bias_b", [P, P], F32)
        wp = sb("wp", [P, P], F32)
        srow = sb("srow", [1, 2 * HD], F32)
        flags = sb("flags", [1, 4], F32)
        flags_i = sb("flags_i", [1, 2], I32)
        eps_c = sb("eps_c", [P, 1], F32)
        ones_c = sb("ones_c", [P, 1], F32)
        mhalf = sb("mhalf", [P, TILES], F32)
        zero16 = sb("zero16", [PARTS * HEADS, CH], BF16)

        ka = sb("ka", [KROWS, 2, HG, SEQ], BF16)
        qa = sb("qa", [KROWS, 2, HG, CH], BF16)
        va = sb("va", [P, 2, KT, HG, VW], F32)
        v_all = sb("v_all", [P, BATCH, NG, KT, HG, VW], F32)
        probs = sb("probs", [P, 4, HG, CH], F32)
        parts = sb("parts", [P, 2, PARTS, 2 * CH], BF16)

        oT = sb("oT", [P, 2, CH], F32)
        rden = sb("rden", [P, TILES, HG], F32)
        attn = sb("attn", [P, TILES, P], F32)
        r1 = sb("r1", [P, TILES, P], F32)
        stats = sb("stats", [P, TILES, 6], F32)
        mv = sb("mv", [P, TILES, 2], F32)
        ve = sb("ve", [P, TILES], F32)
        rs = sb("rs", [P, TILES], F32)

        NW = 2 * HID + 2 * HM * HID + HM * P
        W1, W2, H1, H2, W3 = 0, HID, 2 * HID, 2 * HID + HM * HID, 2 * HID + 2 * HM * HID
        ffn = sb("ffn", [P, 3 * HM * CH], F32)
        w_raw = ffn[:, 0:NW]
        pre_a = ffn[:, 0:HM * CH]
        pre_b = ffn[:, HM * CH:2 * HM * CH]
        act_o = ffn[:, 2 * HM * CH:3 * HM * CH]
        w_hi = sb("w_hi", [P, NW], F32R)
        w_lo = sb("w_lo", [P, NW], F32R)
        x_hi = sb("x_hi", [P, CH], F32R)
        x_lo = sb("x_lo", [P, CH], F32R)
        g_hi = sb("g_hi", [P, HM, CH], F32R)
        g_lo = sb("g_lo", [P, HM, CH], F32R)

        prep = probs[:].rearrange("p a h q -> p (a h q)")
        W2K = 2 * CH
        sq, lnv, rinv, rot_a, rot_b, hn, res = (prep[:, i * W2K:(i + 1) * W2K] for i in range(7))

        MT = HG * KT
        a_flat = attn[:].rearrange("p t c -> p (t c)")
        neg_max, max_res, max_parts = a_flat[:, 0:MT], a_flat[:, MT:2 * MT], a_flat[:, 2 * MT:5 * MT]
        max_row = oT[0:PARTS * MT, 0, 0:P // 2].bitcast(BF16)
        part16 = oT[:, 1, 0:MT // 2].bitcast(BF16)

        ps = ctx.enter_context(nc.psum_tensor("ps", [P, 8, CH], F32))
        S_BANK, O_BANK, MIX_BANK = 0, 4, 6

        in_w = sem("in_w")
        in_x = [sem(f"in_x{t}") for t in range(NCH)]
        in_rope = sem("in_rope")
        in_small = sem("in_small")
        in_res = sem("in_res")
        in_ffn = sem("in_ffn")
        zeros_set = sem("zeros_set")
        consts = sem("consts")
        v_ones = sem("v_ones")
        rows_set = sem("rows_set")
        shift_zero = sem("shift_zero")
        qk_proj = sem("qk_proj")
        v_proj = sem("v_proj")
        sq_done = sem("sq_done")
        var_ready = sem("var_ready")
        ln_done = sem("ln_done")
        rinv_done = sem("rinv_done")
        rot_done = sem("rot_done")
        h_done = sem("h_done")
        p1_done = sem("p1_done")
        res_done = sem("res_done")
        p2_done = sem("p2_done")
        p3_done = sem("p3_done")
        v_evac = sem("v_evac")
        scr_out = [sem("scr_out0"), sem("scr_out1")]
        aug_in = [sem("aug_in0"), sem("aug_in1")]
        qk_ready = sem("qk_ready")
        exp_done = sem("exp_done")
        pv_done = sem("pv_done")
        o_copied = sem("o_copied")
        mix_ready = sem("mix_ready")
        mix_free = sem("mix_free")
        attn_ready = sem("attn_ready")
        var1 = sem("var_eps_ready")
        rstd = sem("rstd_ready")
        x1_ready = sem("x1_ready")
        xs_ready = sem("x_split_ready")
        pre_ready = sem("pre_ready")
        act_done = sem("act_done")
        g_ready = sem("g_split_ready")
        yT_ready = sem("yT_ready")
        y_ready = sem("y_ready")
        stored = sem("stored")
        yo_free = sem("yo_free")
        w_split = sem("w_split")
        lo_flag = sem("lo_flag")
        res_add = sem("res_add")
        chain = sem("chain")
        bound_flag = sem("bound_flag")
        max_in = sem("max_in")
        max_logits = sem("max_logits")
        max_taken = sem("max_taken")
        max_split = sem("max_split")
        max_turned = sem("max_turned")
        max_rows = sem("max_rows")
        max_stored = sem("max_stored")
        max_chain = sem("max_chain")

        block = ctx.enter_context(nc.Block())

        def s_tile(u):
            return ps[:, S_BANK + 2 * (u % 2):S_BANK + 2 * (u % 2) + 2, :]

        @block.sync
        def _(sp):
            sp.dma_start(wq[:], w_qkv).then_inc(in_w, 16)
            for t in range(2):
                sp.dma_start(xT[:, t * CH:(t + 1) * CH], x_t[:, t * CH:(t + 1) * CH]).then_inc(in_x[t], 16)
            sp.dma_start(col[:], cols).then_inc(in_small, 16)
            sp.dma_start(mean8[:], means).then_inc(in_small, 16)
            sp.dma_start(srow[:], scale_rows).then_inc(in_small, 16)
            sp.dma_start(cosT, cosines).then_inc(in_rope, 16)
            sp.dma_start(sinT, sines).then_inc(in_rope, 16)
            for t in range(2, NCH):
                sp.dma_start(xT[:, t * CH:(t + 1) * CH], x_t[:, t * CH:(t + 1) * CH]).then_inc(in_x[t], 16)
            sp.dma_start(ident[:], eye).then_inc(in_res, 16)
            sp.dma_start(bias_b[:], bias).then_inc(in_res, 16)
            sp.dma_start(wp[:], w_proj).then_inc(in_res, 16)
            sp.dma_start(xb[:], x_n.rearrange("(t p) c -> p t c", p=P)).then_inc(in_res, 16)
            sp.wait_ge(zeros_set, 1)
            for c in range(NCH):
                sp.dma_start(m_scr.rearrange("a h t -> (a h) t")[:, c * CH:(c + 1) * CH], zero16[:]).then_inc(shift_zero, 16)

            def store_parts(t):
                sp.wait_ge(p3_done, t + 1)
                for i in range(5):
                    sp.dma_start(q_scr[:, i * HD:(i + 1) * HD, t * CH:(t + 1) * CH],
                                 parts[:, t % 2, i % PARTS, 0:CH]).then_inc(scr_out[t % 2], 16)
                for i in range(PARTS):
                    sp.dma_start(k_scr[:, i * HD:(i + 1) * HD, t * CH:(t + 1) * CH],
                                 parts[:, t % 2, i, CH:2 * CH]).then_inc(scr_out[t % 2], 16)

            def load_group(c, g, first=False):
                slot = g % 2
                if not first:
                    sp.wait_ge(pv_done, (4 * c + g - 1) * KT)
                b = c // 2
                for s in range(PARTS):
                    sp.dma_start(ka[24 * s:24 * s + 24, slot],
                                 k_scr[HG * g:HG * g + HG, :, bass.ds(b * SEQ, SEQ)].rearrange("h r t -> r h t")).then_inc(aug_in[slot], 16)
                    sp.dma_start(qa[24 * s:24 * s + 24, slot],
                                 q_scr[HG * g:HG * g + HG, HD * s:HD * s + 24, bass.ds(c * CH, CH)].rearrange("h r t -> r h t")).then_inc(aug_in[slot], 16)
                sp.dma_start(qa[MROW:MROW + PARTS, slot],
                             m_scr[:, HG * g:HG * g + HG, bass.ds(c * CH, CH)]).then_inc(aug_in[slot], 16)
                vw = KT * HG * VW
                sp.dma_start(va[:, slot].rearrange("p k h v -> p (k h v)"),
                             v_all[:].rearrange("p b g k h v -> p (b g k h v)")[:, bass.ds(b * NG * vw + g * vw, vw)]).then_inc(aug_in[slot], 16)

            def load_for_max(n, b, g):
                sp.wait_ge(max_split, n + 1)
                for s in range(PARTS):
                    sp.dma_start(ka[24 * s:24 * s + 24, 0],
                                 k_scr[bass.ds(HG * g, HG), 0:24, bass.ds(b * SEQ, SEQ)].rearrange("h r t -> r h t")).then_inc(max_in, 16)
                    for i in range(2):
                        sp.dma_start(qa[24 * s:24 * s + 24, i],
                                     q_scr[bass.ds(HG * g, HG), HD * s:HD * s + 24, bass.ds(b * SEQ + i * CH, CH)].rearrange("h r t -> r h t")).then_inc(max_in, 16)

            store_parts(0)
            store_parts(1)
            sp.wait_ge(v_ones, 1)
            sp.wait_ge(rows_set, 1)
            sp.wait_ge(shift_zero, 16 * NCH)
            sp.wait_ge(bound_flag, 1)
            wide = sp.value_load(flags_i[0:1, 0:1], min_val=0, max_val=1)
            with sp.If(wide == 1):
                store_parts(2)
                store_parts(3)
                sp.wait_ge(scr_out[0], 256)
                sp.wait_ge(scr_out[1], 256)
                with sp.Fori(0, BATCH) as b:
                    with sp.Fori(0, NG) as g:
                        n = NG * b + g
                        load_for_max(n, b, g)
                        sp.wait_ge(max_rows, n + 1)
                        for i in range(PARTS):
                            sp.dma_start(m_scr[i, bass.ds(HG * g, HG), bass.ds(b * SEQ, SEQ)],
                                         max_row[i * MT:(i + 1) * MT, :]).then_inc(max_stored, 16)
                sp.wait_ge(max_stored, 16 * PARTS * BATCH * NG)
            sp.wait_ge(v_evac, 2)
            sp.wait_ge(scr_out[0], 128)
            sp.wait_ge(scr_out[1], 128)
            load_group(0, 0, True)
            load_group(0, 1, True)
            with sp.If(wide == 0):
                store_parts(2)
                store_parts(3)
            for src, at in ((w1, W1), (w2, W2), (w3, W3)):
                if at == W3:
                    sp.dma_start(w_raw[:, at:at + HM * P].rearrange("p (k o) -> p k o", k=HM),
                                 src.rearrange("(k p) o -> p k o", p=P)).then_inc(in_ffn, 16)
                else:
                    sp.dma_start(w_raw[:, at:at + HID], src).then_inc(in_ffn, 16)
            for src, at in ((h1, H1), (h2, H2)):
                sp.dma_start(w_raw[:, at:at + HM * HID].rearrange("p (k o) -> p k o", k=HM),
                             src.rearrange("(k p) o -> p k o", p=P)).then_inc(in_ffn, 16)
            load_group(0, 2)
            load_group(0, 3)
            sp.wait_ge(v_evac, 4)
            sp.wait_ge(scr_out[0], 256)
            sp.wait_ge(scr_out[1], 256)
            with sp.Fori(1, NCH) as c:
                for g in range(NG):
                    load_group(c, g)

        @block.gpsimd
        def _(pool):
            pool.memset(zero16[:], 0.0).then_inc(zeros_set, 1)
            pool.memset(mhalf[:], -0.5)
            pool.memset(va[:], 1.0)
            pool.memset(v_all[:], 1.0).then_inc(v_ones, 1)
            pool.wait_ge(in_res, 64)
            pool.tensor_tensor(xb[:], xb[:], bias_b[:, None, :].to_broadcast([P, NCH * TILES, P]), ALU.add).then_inc(res_add, 1)

            def rsqrt(n):
                pool.wait_ge(var1, n + 1)
                pool.tensor_tensor(rs[:], ve[:], mhalf[:], ALU.pow).then_inc(rstd, 1)

            def finish(c):
                rsqrt(2 * c)
                rsqrt(2 * c + 1)
                pool.wait_ge(y_ready, c + 1)
                pool.dma_start(out.rearrange("(t p) c -> p t c", p=P)[:, bass.ds(c * TILES, TILES), :], yo).then_inc(stored, 16)
                pool.wait_ge(stored, 16 * (c + 1))
                pool.nop().then_inc(yo_free, 1)

            pool.nop().then_inc(yo_free, 1)
            with pool.Fori(0, NCH) as c:
                finish(c)

        @block.tensor
        def _(pe):
            def prepare(t):
                pe.wait_ge(in_x[t], 16)
                wait(pe, rot_done, t)
                wait(pe, sq_done, t)
                for i in range(4):
                    mm = pe.matmul(ps[:, i, :], wq[:, i * P:(i + 1) * P], xT[:, t * CH:(t + 1) * CH], start=True, stop=True)
                mm.then_inc(qk_proj, 1)
                wait(pe, v_evac, t - 1)
                for i in range(TILES):
                    mm = pe.matmul(ps[:, 6 + t % 2, i * P:(i + 1) * P], xT[:, t * CH + i * P:t * CH + (i + 1) * P],
                                   wq[:, 4 * P:5 * P], start=True, stop=True)
                mm.then_inc(v_proj, 1)
                pe.wait_ge(sq_done, t + 1)
                wait(pe, ln_done, t)
                for i in range(2):
                    mm = pe.matmul(ps[:, 4 + i, :], mean8[:], sq[:, i * CH:(i + 1) * CH], start=True, stop=True)
                mm.then_inc(var_ready, 1)

            def logits(c, step, pair):
                g, kt = divmod(step, KT)
                slot = g % 2
                if kt == 0 and pair == 0:
                    pe.wait_ge(aug_in[slot], 128 * (2 * c + g // 2 + 1))
                u = 2 * step + pair
                wait(pe, exp_done, 64 * c + u - 1)
                for i in range(2):
                    h = 2 * pair + i
                    mm = pe.matmul(s_tile(u)[:, i, :], ka[:, slot, h, kt * P:(kt + 1) * P], qa[:, slot, h, :], start=True, stop=True)
                mm.then_inc(qk_ready, 1)

            def values(c, step):
                g, kt = divmod(step, KT)
                pe.wait_ge(exp_done, 64 * c + 2 * step + 2)
                if kt == 0:
                    wait(pe, o_copied, 4 * c + g - 1)
                for h in range(HG):
                    mm = pe.matmul(ps[32 * h:32 * h + VW, O_BANK + g % 2, :], va[:, g % 2, kt, h, :], probs[:, step % 4, h, :],
                                   start=(kt == 0), stop=(kt == KT - 1))
                mm.then_inc(pv_done, 1)

            use = [0, 0]

            def mix(base):
                n = use[1]
                use[1] += 1
                wait(pe, mix_free, base + n - 1)
                return ps[:, MIX_BANK + (n + use[0]) % 2, :]

            def o_transpose(base, c, g):
                bank = mix(base)
                pe.wait_ge(o_copied, 4 * c + g + 1)
                for i in range(TILES):
                    mm = pe.transpose(bank[:, i * P:(i + 1) * P], oT[:, g % 2, i * P:(i + 1) * P], ident[:])
                mm.then_inc(mix_ready, 1)

            def project(base, c, stage):
                if stage < 2:
                    bank = mix(base)
                    pe.wait_ge(attn_ready, 4 * c + 4)
                    for i in range(2):
                        mm = pe.transpose(bank[:, i * P:(i + 1) * P], attn[:, 2 * stage + i, :], ident[:])
                else:
                    pe.wait_ge(mix_free, base + use[1])
                    bank = mix(base)
                    for i in range(TILES):
                        mm = pe.matmul(bank[:, i * P:(i + 1) * P], attnT[:, i * P:(i + 1) * P], wp[:], start=True, stop=True)
                mm.then_inc(mix_ready, 1)

            def x_transpose(base, c):
                bank = mix(base)
                pe.wait_ge(x1_ready, c + 1)
                for i in range(TILES):
                    mm = pe.transpose(bank[:, i * P:(i + 1) * P], x1[:, i, :], ident[:])
                mm.then_inc(mix_ready, 1)

            def split_products(bank, terms, passes):
                todo = [(w, x) for w_hl, x_hl in terms for w in w_hl[:1 + (passes > 2)] for x in x_hl]
                for i, (w, x) in enumerate(todo):
                    mm = pe.matmul(bank, w, x, start=(i == 0), stop=(i == len(todo) - 1))
                mm.then_inc(mix_ready, 1)

            def w_at(col0):
                return w_hi[:, col0:col0 + P], w_lo[:, col0:col0 + P]

            def up(base, c, m, passes):
                for w in (W1, W2):
                    bank = mix(base)
                    pe.wait_ge(xs_ready, c + 1)
                    split_products(bank, [(w_at(w + m * P), (x_hi[:], x_lo[:]))], passes)

            def hidden(base, c, layer, m, passes):
                bank = mix(base)
                pe.wait_ge(g_ready, 3 * c + 1 + layer)
                w = (H1, H2)[layer]
                split_products(bank, [(w_at(w + k * HID + m * P), (g_hi[:, k, :], g_lo[:, k, :])) for k in range(HM)], passes)

            def down(base, c, passes):
                bank = mix(base)
                pe.wait_ge(g_ready, 3 * c + 3)
                split_products(bank, [(w_at(W3 + k * P), (g_hi[:, k, :], g_lo[:, k, :])) for k in range(HM)], passes)

            def y_transpose(base, c):
                bank = mix(base)
                pe.wait_ge(yT_ready, c + 1)
                for i in range(TILES):
                    mm = pe.transpose(bank[:, i * P:(i + 1) * P], yT[:, i * P:(i + 1) * P], ident[:])
                mm.then_inc(mix_ready, 1)

            def ffn_at(base, c, step, passes):
                if step == 1:
                    o_transpose(base, c, NG - 1)
                if step == 2:
                    project(base, c, 0)
                    project(base, c, 1)
                if step == 3:
                    project(base, c, 2)
                if step == 6:
                    x_transpose(base, c)
                if 8 <= step < 12:
                    up(base, c, step - 8, passes)
                if 16 <= step < 20:
                    hidden(base, c, 0, step - 16, passes)
                if 23 <= step < 27:
                    hidden(base, c, 1, step - 23, passes)
                if step == 30:
                    down(base, c, passes)
                if step == 31:
                    y_transpose(base, c)

            def chunk(c, passes):
                base = 0 if passes == 0 else MIX_CHUNK * (c - 1) + MIX_FIRST
                use[0], use[1] = (0, 0) if passes == 0 else (MIX_FIRST, 0)
                for step in range(STEPS):
                    logits(c, step, 0)
                    logits(c, step, 1)
                    if step:
                        values(c, step - 1)
                    elif passes:
                        values(c - 1, STEPS - 1)
                    if passes:
                        ffn_at(base, c - 1, step, passes)
                    if step in (KT + 1, 2 * KT + 1, 3 * KT + 1):
                        o_transpose(base, c, step // KT - 1)

            def later_chunks(passes):
                with pe.Fori(1, NCH) as c:
                    chunk(c, passes)
                    assert use[1] == MIX_CHUNK
                base = MIX_CHUNK * (NCH - 1) + MIX_FIRST
                use[0], use[1] = MIX_FIRST, 0
                values(NCH - 1, STEPS - 1)
                for step in range(STEPS):
                    ffn_at(base, NCH - 1, step, passes)

            pe.wait_ge(in_w, 16)
            pe.wait_ge(in_small, 48)
            for t in range(NCH):
                prepare(t)
            pe.wait_ge(rot_done, NCH)
            pe.wait_ge(ln_done, NCH)
            pe.wait_ge(v_evac, NCH)
            pe.wait_ge(rows_set, 2)
            pe.wait_ge(in_res, 64)

            def row_maxima(n):
                pe.wait_ge(max_in, 144 * (n + 1))
                for u in range(MT):
                    h, t = divmod(u, KT)
                    if u >= 2:
                        pe.wait_ge(max_taken, MT * n + u - 1)
                    for i in range(2):
                        mm = pe.matmul(s_tile(u)[:, i, :], qa[:, t // TILES, h, (t % TILES) * P:(t % TILES + 1) * P],
                                       ka[:, 0, h, i * CH:(i + 1) * CH], start=True, stop=True)
                    mm.then_inc(max_logits, 1)
                pe.wait_ge(max_split, n + 2)
                pe.transpose(ps[0:PARTS * MT, MIX_BANK, 0:P], max_parts, ident[:]).then_inc(max_turned, 1)

            pe.wait_ge(bound_flag, 1)
            wide = pe.value_load(flags_i[0:1, 0:1], min_val=0, max_val=1)
            with pe.If(wide == 1):
                with pe.Fori(0, BATCH * NG) as n:
                    row_maxima(n)
                pe.wait_ge(max_rows, BATCH * NG)

            chunk(0, 0)
            bank = mix(0)
            pe.wait_ge(w_split, 1)
            pe.matmul(bank[0:1, 0:1], ve[:, 0:1], ones_c[:], start=True, stop=True).then_inc(mix_ready, 1)
            pe.wait_ge(lo_flag, 1)
            low = pe.value_load(flags_i[0:1, 1:2], min_val=0, max_val=1)
            with pe.If(low == 0):
                later_chunks(2)
            with pe.If(low == 1):
                later_chunks(4)

        @block.scalar
        def _(act):
            act.wait_ge(consts, 1)
            for t in range(NCH):
                act.wait_ge(qk_proj, t + 1)
                wait(act, var_ready, t)
                nc.scalar.activation(sq, ps[:, 0:2, :].rearrange("p a q -> p (a q)"), ACT.Square).then_inc(sq_done, 1)
                act.wait_ge(var_ready, t + 1)
                wait(act, rinv_done, t)
                nc.scalar.activation(lnv, ps[:, 4:6, :].rearrange("p a q -> p (a q)"), ACT.Ln, bias=eps_c[:]).then_inc(ln_done, 1)
                act.wait_ge(ln_done, t + 1)
                wait(act, h_done, t)
                nc.scalar.activation(rinv, lnv, ACT.Exp, scale=-0.5).then_inc(rinv_done, 1)
                act.wait_ge(h_done, t + 1)
                if t >= 2:
                    act.wait_ge(scr_out[t % 2], 128)
                nc.scalar.copy(parts[:, t % 2, 0, :], hn).then_inc(p1_done, 1)
                act.wait_ge(res_done, t + 1)
                nc.scalar.copy(parts[:, t % 2, 1, :], res).then_inc(p2_done, 1)

            act.wait_ge(p3_done, NCH)

            def exps(c, step):
                for pair in range(2):
                    u = 2 * step + pair
                    act.wait_ge(qk_ready, 64 * c + u + 1)
                    if pair == 0:
                        wait(act, pv_done, 32 * c + step - 3)
                    nc.scalar.activation(probs[:, step % 4, 2 * pair:2 * pair + 2, :], s_tile(u), ACT.Exp).then_inc(exp_done, 1)

            def activate(c, layer):
                act.wait_ge(pre_ready, 3 * c + layer + 1)
                nc.scalar.activation(act_o, pre_a, (ACT.Silu, ACT.Gelu, ACT.Gelu)[layer]).then_inc(act_done, 1)

            for step in range(STEPS):
                exps(0, step)
            with act.Fori(1, NCH) as c:
                for step in range(STEPS):
                    exps(c, step)
                    if step in (12, 20, 27):
                        activate(c - 1, (12, 20, 27).index(step))
            for layer in range(3):
                activate(NCH - 1, layer)

        @block.vector
        def _(dve):
            links = [0]

            def link(ins, base):
                links[0] += 1
                ins.then_inc(chain, 1)
                dve.wait_ge(chain, base + links[0])

            nc.vector.memset(eps_c[:], EPS_RMS)
            nc.vector.memset(ones_c[:], 1.0).then_inc(consts, 1)
            nc.vector.memset(ka[64:96], 1.0)
            nc.vector.memset(qa[64:96], 0.0).then_inc(rows_set, 1)
            dve.wait_ge(in_small, 48)
            for i in range(2):
                ins = nc.vector.tensor_reduce(flags[:, i:i + 1], srow[:, i * HD:(i + 1) * HD], AX.X, ALU.max, apply_absolute_value=True)
            link(ins, 0)
            link(nc.vector.tensor_scalar(flags[:, 2:3], flags[:, 0:1], flags[:, 1:2], HD ** 0.5, ALU.mult, ALU.mult), 0)
            link(nc.vector.tensor_scalar(flags[:, 3:4], flags[:, 2:3], LOGIT_BOUND, None, ALU.is_gt), 0)
            nc.vector.tensor_copy(flags_i[:, 0:1], flags[:, 3:4]).then_inc(bound_flag, 1)
            link(nc.vector.tensor_scalar(col[:, C_Q:C_QS + 1], col[:, C_Q:C_QS + 1], HD ** -0.5, None, ALU.mult), 0)
            dve.wait_ge(in_rope, 32)
            for t in range(NCH):
                half = (t % 2) * CH
                dve.wait_ge(qk_proj, t + 1)
                for i, c_, table, dst in ((2, C_QS, sinT, rot_b), (3, C_KS, sinT, rot_b), (0, C_Q, cosT, rot_a), (1, C_K, cosT, rot_a)):
                    if i == 0:
                        dve.wait_ge(sq_done, t + 1)
                    ins = nc.vector.scalar_tensor_tensor(
                        out=dst[:, (i % 2) * CH:(i % 2 + 1) * CH], in0=ps[:, i, :], scalar=col[:, c_:c_ + 1],
                        in1=table[:, half:half + CH], op0=ALU.mult, op1=ALU.mult)
                ins.then_inc(rot_done, 1)
                dve.wait_ge(rot_done, t + 1)
                link(nc.vector.tensor_tensor(rot_a, rot_a, rot_b, ALU.add), 0)
                dve.wait_ge(rinv_done, t + 1)
                wait(dve, p1_done, t)
                nc.vector.tensor_tensor(hn, rot_a, rinv, ALU.mult).then_inc(h_done, 1)
                dve.wait_ge(v_proj, t + 1)
                if t == 0:
                    dve.wait_ge(v_ones, 1)
                for i in range(TILES):
                    kt = (t % 2) * TILES + i
                    ins = nc.vector.tensor_copy(v_all[:, t // 2, :, kt, :, 0:HD],
                                                ps[:, 6 + t % 2, i * P:(i + 1) * P].rearrange("p (g h d) -> p g h d", g=NG, h=HG))
                ins.then_inc(v_evac, 1)
                dve.wait_ge(p1_done, t + 1)
                dve.wait_ge(h_done, t + 1)
                wait(dve, p3_done, t)
                nc.vector.tensor_tensor(res, hn, parts[:, t % 2, 0, :], ALU.subtract).then_inc(res_done, 1)
                dve.wait_ge(p2_done, t + 1)
                nc.vector.tensor_tensor(parts[:, t % 2, 2, :], res, parts[:, t % 2, 1, :], ALU.subtract).then_inc(p3_done, 1)
            dve.wait_ge(bound_flag, 1)
            dve.wait_ge(ln_done, NCH)
            nc.vector.memset(ps[:, O_BANK:O_BANK + 2, :], 0.0).then_inc(rows_set, 1)

            use = [0]

            def mixed(base):
                n = use[0]
                use[0] += 1
                dve.wait_ge(mix_ready, base + n + 1)
                return n

            def bank_of(n, first):
                return ps[:, MIX_BANK + (n + first) % 2, :]

            def copy_o(c, g):
                dve.wait_ge(pv_done, KT * (4 * c + g + 1))
                nc.vector.tensor_copy(oT[:, g % 2, :], ps[:, O_BANK + g % 2, :]).then_inc(o_copied, 1)

            def normalise(base, cb, c, g, first):
                n = mixed(base)
                bank = bank_of(n, first).rearrange("p (t h r) -> p t h r", t=TILES, h=HG)
                link(nc.vector.reciprocal(rden[:], bank[:, :, :, HD]), cb)
                dst = attn[:, :, g * 32:(g + 1) * 32].rearrange("p t (h d) -> p t h d", h=HG)
                nc.vector.tensor_tensor(dst, bank[:, :, :, 0:HD], rden[:, :, :, None].to_broadcast([P, TILES, HG, HD]),
                                        ALU.mult).then_inc(mix_free, 1)
                dve.wait_ge(mix_free, base + n + 1)
                dve.nop().then_inc(attn_ready, 1)

            def layer_norm(cb, src, dst):
                for i in range(TILES):
                    ins = nc.vector.bn_stats(stats[:, i, :], src[:, i, :])
                link(ins, cb)
                nc.vector.memset(ve[:], 0.0)
                for i in range(TILES):
                    ins = nc.vector.bn_aggr(mv[:, i, :], stats[:, i, :])
                link(ins, cb)
                nc.vector.tensor_scalar(ve[:], mv[:, :, 1], EPS_LN, None, ALU.add).then_inc(var1, 1)

            def scale_rows_of(n, src, dst):
                dve.wait_ge(rstd, n)
                for i in range(TILES):
                    ins = nc.vector.tensor_scalar(dst[:, i, :], src[:, i, :], mv[:, i, 0:1], rs[:, i:i + 1],
                                                  ALU.subtract, ALU.mult)
                return ins

            def split(cb, src, hi, lo):
                link(nc.vector.tensor_copy(hi, src), cb)
                return nc.vector.tensor_tensor(lo, src, hi.bitcast(F32), ALU.subtract)

            def ffn_at(base, cb, c, step, first):
                if step == 1:
                    normalise(base, cb, c, NG - 1, first)
                if step == 2:
                    for i in range(2):
                        n = mixed(base)
                        nc.vector.tensor_copy(attnT[:, i * 2 * P:(i + 1) * 2 * P], bank_of(n, first)[:, 0:2 * P]).then_inc(mix_free, 1)
                if step == 3:
                    n = mixed(base)
                    r = r1[:].rearrange("p t c -> p (t c)")
                    xr = xb[:].rearrange("p t c -> p (t c)")[:, bass.ds(c * CH, CH)]
                    nc.vector.tensor_tensor(r, bank_of(n, first), xr, ALU.add).then_inc(mix_free, 1)
                    dve.wait_ge(mix_free, base + n + 1)
                    layer_norm(cb, r1, x1)
                    scale_rows_of(2 * c + 1, r1, x1).then_inc(x1_ready, 1)
                if step == 6:
                    n = mixed(base)
                    split(cb, bank_of(n, first), x_hi[:], x_lo[:]).then_inc(mix_free, 1)
                    dve.wait_ge(mix_free, base + n + 1)
                    dve.nop().then_inc(xs_ready, 1)
                if 8 <= step < 12:
                    m = step - 8
                    for c0, dst in ((C_S1, pre_a), (C_S2, pre_b)):
                        n = mixed(base)
                        ins = nc.vector.tensor_scalar(dst[:, m * CH:(m + 1) * CH], bank_of(n, first), col[:, c0 + m:c0 + m + 1],
                                                      None, ALU.mult)
                        ins.then_inc(mix_free, 1)
                    if m == HM - 1:
                        dve.wait_ge(mix_free, base + n + 1)
                        dve.nop().then_inc(pre_ready, 1)
                for layer, s0 in ((0, 16), (1, 23)):
                    if s0 <= step < s0 + HM:
                        m = step - s0
                        n = mixed(base)
                        nc.vector.tensor_scalar(pre_a[:, m * CH:(m + 1) * CH], bank_of(n, first),
                                                col[:, (C_H1, C_H2)[layer] + m:(C_H1, C_H2)[layer] + m + 1],
                                                None, ALU.mult).then_inc(mix_free, 1)
                        if m == HM - 1:
                            dve.wait_ge(mix_free, base + n + 1)
                            dve.nop().then_inc(pre_ready, 1)
                gh, gl = g_hi[:].rearrange("p k q -> p (k q)"), g_lo[:].rearrange("p k q -> p (k q)")
                if step == 12:
                    dve.wait_ge(act_done, 3 * c + 1)
                    link(nc.vector.tensor_tensor(act_o, act_o, pre_b, ALU.mult), cb)
                    split(cb, act_o, gh, gl).then_inc(g_ready, 1)
                if step in (20, 27):
                    dve.wait_ge(act_done, 3 * c + 2 + (step == 27))
                    split(cb, act_o, gh, gl).then_inc(g_ready, 1)
                if step == 30:
                    n = mixed(base)
                    nc.vector.tensor_scalar(yT, bank_of(n, first), col[:, C_W3:C_W3 + 1], None, ALU.mult).then_inc(mix_free, 1)
                    dve.wait_ge(mix_free, base + n + 1)
                    dve.nop().then_inc(yT_ready, 1)
                if step == 31:
                    n = mixed(base)
                    nc.vector.tensor_tensor(r1[:].rearrange("p t c -> p (t c)"), bank_of(n, first),
                                            x1.rearrange("p t c -> p (t c)"), ALU.add).then_inc(mix_free, 1)
                    dve.wait_ge(mix_free, base + n + 1)
                    layer_norm(cb, r1, yo)
                    dve.wait_ge(yo_free, c + 1)
                    scale_rows_of(2 * c + 2, r1, yo).then_inc(y_ready, 1)

            def chunk(c, base, cb, first, with_ffn):
                for step in range(STEPS):
                    g, kt = divmod(step, KT)
                    if kt == 0 and g:
                        copy_o(c, g - 1)
                    if kt == 0 and g == 0 and with_ffn:
                        copy_o(c - 1, NG - 1)
                    if with_ffn:
                        ffn_at(base, cb, c - 1, step, first)
                    if kt == 1 and g:
                        normalise(base, cb, c, g - 1, first)

            def max_link(ins, n, k):
                ins.then_inc(max_chain, 1)
                dve.wait_ge(max_chain, 5 * n + k)

            def row_maxima(n):
                for u in range(MT):
                    dve.wait_ge(max_logits, MT * n + u + 1)
                    ins = nc.vector.tensor_reduce(neg_max[:, u:u + 1], s_tile(u).rearrange("p a q -> p (a q)"), AX.X, ALU.max, negate=True)
                    ins.then_inc(max_taken, 1)
                dve.wait_ge(max_taken, MT * (n + 1))
                src = neg_max
                for i in range(PARTS):
                    max_link(nc.vector.tensor_copy(part16, src), n, 2 * i + 1)
                    if i < PARTS - 1:
                        nc.vector.tensor_copy(max_parts[:, i * MT:(i + 1) * MT], part16)
                        max_link(nc.vector.tensor_tensor(max_res, src, part16, ALU.subtract), n, 2 * i + 2)
                    else:
                        nc.vector.tensor_copy(max_parts[:, i * MT:(i + 1) * MT], part16).then_inc(max_split, 1)
                    src = max_res
                dve.wait_ge(max_turned, n + 1)
                nc.vector.tensor_copy(max_row, ps[0:PARTS * MT, MIX_BANK, 0:P]).then_inc(max_rows, 1)
                dve.wait_ge(max_stored, 16 * PARTS * (n + 1))

            wide = dve.value_load(flags_i[0:1, 0:1], min_val=0, max_val=1)
            with dve.If(wide == 1):
                dve.nop().then_inc(max_split, 1)
                with dve.Fori(0, BATCH * NG) as n:
                    row_maxima(n)

            dve.wait_ge(in_ffn, 80)
            link(nc.vector.tensor_copy(w_hi[:], w_raw), 0)
            link(nc.vector.tensor_tensor(w_lo[:], w_raw, w_hi[:].bitcast(F32), ALU.subtract), 0)
            nc.vector.tensor_reduce(ve[:, 0:1], w_lo[:].bitcast(F32), AX.X, ALU.max, apply_absolute_value=True).then_inc(w_split, 1)
            chunk(0, 0, 0, 0, False)
            n = mixed(0)
            link(nc.vector.tensor_scalar(flags[:, 0:1], bank_of(n, 0)[0:1, 0:1], 0.0, None, ALU.not_equal), 0)
            nc.vector.tensor_copy(flags_i[:, 1:2], flags[:, 0:1]).then_inc(lo_flag, 1)
            dve.nop().then_inc(mix_free, 1)
            dve.wait_ge(res_add, 1)
            start = links[0]
            with dve.Fori(1, NCH) as c:
                use[0], links[0] = 0, 0
                chunk(c, MIX_CHUNK * (c - 1) + MIX_FIRST, CHAIN_CHUNK * (c - 1) + start, MIX_FIRST, True)
                assert use[0] == MIX_CHUNK and links[0] == CHAIN_CHUNK
            use[0], links[0] = 0, 0
            copy_o(NCH - 1, NG - 1)
            for step in range(STEPS):
                ffn_at(MIX_CHUNK * (NCH - 1) + MIX_FIRST, CHAIN_CHUNK * (NCH - 1) + start, NCH - 1, step, MIX_FIRST)


def kernel(**inputs):
    import concourse.bacc as bacc
    from concourse.bass_utils import run_bass_kernel_spmd

    a = {k.split("_", 1)[1]: np.ascontiguousarray(v) for k, v in inputs.items()}
    x = a["attn_x"].reshape(TOK, DIM)
    swap = (np.arange(DIM) // HD) * HD + (np.arange(DIM) + HD // 2) % HD
    w = a["attn_w_qkv"]
    w_q, w_k, w_v = w[:, :DIM], w[:, DIM:2 * DIM], w[:, 2 * DIM:]
    d_of = np.arange(DIM) % HD
    q_s, k_s = a["attn_q_scale"][d_of], a["attn_k_scale"][d_of]
    by_tile = lambda s: s.reshape(HM, P).T
    half = HD // 2
    freqs = (np.float32(1.0) / np.float32(1250) ** (np.arange(half, dtype=np.float32) / np.float32(half))).astype(np.float32)
    angle = np.outer(np.arange(SEQ, dtype=np.float32), freqs).astype(np.float32)[:, d_of % half].T
    sign = np.where(d_of < half, -1.0, 1.0).astype(np.float32)[:, None]
    same_head = np.arange(P)[:, None] // HD == np.arange(P)[None, :] // HD
    arrays = {
        "x_t": x.T, "x_n": x,
        "w_qkv": np.concatenate([w_q, w_k, w_q[:, swap], w_k[:, swap], w_v], axis=1),
        "cols": np.concatenate([by_tile(a["ffn_w1_s"]), by_tile(a["ffn_w2_s"]), by_tile(a["ffn_h1_s"]), by_tile(a["ffn_h2_s"]),
                                a["ffn_w3_s"][:, None], q_s[:, None], q_s[swap][:, None], k_s[:, None], k_s[swap][:, None]], axis=1),
        "scale_rows": np.concatenate([a["attn_q_scale"], a["attn_k_scale"]])[None, :],
        "bias": np.broadcast_to(a["attn_b_proj"][None, :], (P, DIM)),
        "w_proj": a["attn_w_proj"],
        "w1": a["ffn_w1_w"].T, "w2": a["ffn_w2_w"].T, "h1": a["ffn_h1_w"].T, "h2": a["ffn_h2_w"].T, "w3": a["ffn_w3_w"].T,
        "cosines": np.cos(angle).astype(np.float32), "sines": (np.sin(angle) * sign).astype(np.float32),
        "means": (same_head / HD).astype(np.float32), "eye": np.eye(P, dtype=np.float32),
    }
    nc = bacc.Bacc("TRN2", target_bir_lowering=False, num_devices=1)
    sent, args = {}, []
    for name, v in arrays.items():
        v = np.ascontiguousarray(v)
        sent[f"in_{name}"] = v
        args.append(nc.dram_tensor(f"in_{name}", v.shape, mybir.dt.from_np(v.dtype), kind="ExternalInput").ap())
    out = nc.dram_tensor("out_y", (TOK, DIM), F32, kind="ExternalOutput").ap()
    build(nc, *args, out)
    r = run_bass_kernel_spmd(nc, [sent], core_ids=[0])
    return r.results[0]["out_y"].reshape(BATCH, SEQ, DIM)
```

```python
from contextlib import ExitStack

import numpy as np

import concourse.bass as bass
from concourse import mybir

F32 = mybir.dt.float32
F32R = mybir.dt.float32r
BF16 = mybir.dt.bfloat16
I32 = mybir.dt.int32
ALU = mybir.AluOpType
ACT = mybir.ActivationFunctionType
AX = mybir.AxisListType

P = 128
BATCH, SEQ, DIM = 2, 1024, 128
HEADS, HD = 16, 8
TOK = BATCH * SEQ
HID = 512
CH = 512
NCH = TOK // CH
TILES = CH // P
HG = 4
NG = HEADS // HG
KT = SEQ // P
STEPS = NG * KT
PARTS = 3
MROW = PARTS * PARTS * HD
KROWS = P
HM = HID // P
VW = HD + 1
EPS_RMS, EPS_LN = 1e-6, 1e-5
LOGIT_BOUND = 60.0

MIX_FIRST = 4
MIX_CHUNK = 25
CHAIN_CHUNK = 25

C_S1, C_S2, C_H1, C_H2, C_W3 = 0, 4, 8, 12, 16
C_Q, C_QS, C_K, C_KS = 17, 18, 19, 20
NCOL = 21
C_S2H = NCOL
WARM = 20
SLOTS = 2 * STEPS
UP_SLOTS = (16, 18, 21, 23, 25, 27, 29, 31)
GATE_STEPS = (10, 12, 14, 16)
GATE_SLOTS = (24, 28, 32, 36)
HIDDEN_SLOTS = ((38, 40, 42, 43), (47, 48, 50, 51))
GELU_STEPS = (21, 25)
SPLIT_SLOTS = (44, 52)
X_SLOT, DOWN_SLOT, Y_SLOT = 13, 56, 58
O_SLOTS = (19, 35, 61)


def wait(eng, sem, count):
    if isinstance(count, int) and count <= 0:
        return
    eng.wait_ge(sem, count)


def build(nc, x_t, x_n, w_qkv, cols, scale_rows, bias, w_proj, w1, w2, h1, h2, w3, cosines, sines, means, eye, out):
    ctx = ExitStack()
    with ctx:
        def sb(name, shape, dt):
            return ctx.enter_context(nc.sbuf_tensor(name, shape, dt))

        def sem(name):
            return ctx.enter_context(nc.semaphore(name))

        q_scr = nc.dram_tensor("q_scr", [HEADS, 5 * HD, TOK], BF16).ap()
        k_scr = nc.dram_tensor("k_scr", [HEADS, 3 * HD, TOK], BF16).ap()
        m_scr = nc.dram_tensor("m_scr", [PARTS, HEADS, TOK], BF16).ap()

        xT = sb("xT", [P, TOK], F32)
        xb = sb("xb", [P, NCH * TILES, P], F32)
        wq = sb("wq", [P, 5 * P], F32)
        col = sb("col", [P, NCOL + HM], F32)
        rope = sb("rope", [P, 4 * CH], F32)
        cosT, sinT = rope[:, 0:SEQ], rope[:, SEQ:2 * SEQ]
        attnT, yT = rope[:, 0:CH], rope[:, CH:2 * CH]
        x1, yo = (rope[:, i * CH:(i + 1) * CH].rearrange("p (t c) -> p t c", t=TILES) for i in (2, 3))
        mean8 = sb("mean8", [P, P], F32)
        ident = sb("ident", [P, P], F32)
        bias_b = sb("bias_b", [P, P], F32)
        wp = sb("wp", [P, P], F32)
        srow = sb("srow", [1, 2 * HD], F32)
        flags = sb("flags", [1, 4], F32)
        flags_i = sb("flags_i", [1, 2], I32)
        eps_c = sb("eps_c", [P, 1], F32)
        ones_c = sb("ones_c", [P, 1], F32)
        mhalf = sb("mhalf", [P, TILES], F32)
        warm = sb("warm", [P, CH], BF16)
        zero16 = sb("zero16", [PARTS * HEADS, CH], BF16)

        ka = sb("ka", [KROWS, 2, HG, SEQ], BF16)
        qa = sb("qa", [KROWS, 2, HG, CH], BF16)
        va = sb("va", [P, 2, KT, HG, VW], F32)
        v_all = sb("v_all", [P, BATCH, NG, KT, HG, VW], F32)
        probs = sb("probs", [P, 4, HG, CH], F32)
        parts = sb("parts", [P, 2, PARTS, 2 * CH], BF16)

        oT = sb("oT", [P, 2, CH], F32)
        rden = sb("rden", [P, TILES, HG], F32)
        attn = sb("attn", [P, TILES, P], F32)
        r1 = sb("r1", [P, TILES, P], F32)
        stats = sb("stats", [P, TILES, 6], F32)
        mv = sb("mv", [P, TILES, 2], F32)
        ve = sb("ve", [P, TILES], F32)
        rs = sb("rs", [P, TILES], F32)

        NW = 2 * HID + 2 * HM * HID + HM * P
        W1, W2, H1, H2, W3 = 0, HID, 2 * HID, 2 * HID + HM * HID, 2 * HID + 2 * HM * HID
        ffn = sb("ffn", [P, 3 * HM * CH], F32)
        w_raw = ffn[:, 0:NW]
        pre_a = ffn[:, 0:HM * CH]
        pre_b = ffn[:, HM * CH:2 * HM * CH]
        act_o = ffn[:, 2 * HM * CH:3 * HM * CH]
        w_hi = sb("w_hi", [P, NW], F32R)
        w_lo = sb("w_lo", [P, NW], F32R)
        x_hi = sb("x_hi", [P, CH], F32R)
        x_lo = sb("x_lo", [P, CH], F32R)
        g_hi = sb("g_hi", [P, HM, CH], F32R)
        g_lo = sb("g_lo", [P, HM, CH], F32R)

        prep = probs[:].rearrange("p a h q -> p (a h q)")
        W2K = 2 * CH
        sq, lnv, rinv, rot_a, rot_b, hn, res = (prep[:, i * W2K:(i + 1) * W2K] for i in range(7))

        MT = HG * KT
        a_flat = attn[:].rearrange("p t c -> p (t c)")
        neg_max, max_res, max_parts = a_flat[:, 0:MT], a_flat[:, MT:2 * MT], a_flat[:, 2 * MT:5 * MT]
        max_row = oT[0:PARTS * MT, 0, 0:P // 2].bitcast(BF16)
        part16 = oT[:, 1, 0:MT // 2].bitcast(BF16)

        ps = ctx.enter_context(nc.psum_tensor("ps", [P, 8, CH], F32))
        O_BANK, MIX_BANK = 6, 7

        in_w = sem("in_w")
        in_x = [sem(f"in_x{t}") for t in range(NCH)]
        in_rope = sem("in_rope")
        in_small = sem("in_small")
        in_res = sem("in_res")
        in_ffn = sem("in_ffn")
        zeros_set = sem("zeros_set")
        consts = sem("consts")
        v_ones = sem("v_ones")
        rows_set = sem("rows_set")
        half_set = sem("half_set")
        o_rows_set = sem("o_rows_set")
        warm_set = sem("warm_set")
        shift_zero = sem("shift_zero")
        qk_proj = sem("qk_proj")
        v_proj = sem("v_proj")
        sq_done = sem("sq_done")
        var_ready = sem("var_ready")
        ln_done = sem("ln_done")
        rinv_done = sem("rinv_done")
        rot_done = sem("rot_done")
        h_done = sem("h_done")
        p1_done = sem("p1_done")
        res_done = sem("res_done")
        p2_done = sem("p2_done")
        p3_done = sem("p3_done")
        v_evac = sem("v_evac")
        scr_out = [sem("scr_out0"), sem("scr_out1")]
        aug_in = [sem("aug_in0"), sem("aug_in1")]
        qk_ready = sem("qk_ready")
        exp_done = sem("exp_done")
        pv_done = sem("pv_done")
        o_copied = sem("o_copied")
        mix_ready = sem("mix_ready")
        mix_free = sem("mix_free")
        attn_ready = sem("attn_ready")
        var1 = sem("var_eps_ready")
        rstd = sem("rstd_ready")
        x1_ready = sem("x1_ready")
        xs_ready = sem("x_split_ready")
        pre_ready = sem("pre_ready")
        act_done = sem("act_done")
        g_ready = sem("g_split_ready")
        yT_ready = sem("yT_ready")
        y_ready = sem("y_ready")
        stored = sem("stored")
        yo_free = sem("yo_free")
        w_split = sem("w_split")
        lo_flag = sem("lo_flag")
        res_add = sem("res_add")
        chain = sem("chain")
        last_up = sem("last_up")
        last_hidden = sem("last_hidden")
        last_act = sem("last_act")
        last_split = sem("last_split")
        bound_flag = sem("bound_flag")
        max_in = sem("max_in")
        max_logits = sem("max_logits")
        max_taken = sem("max_taken")
        max_split = sem("max_split")
        max_turned = sem("max_turned")
        max_rows = sem("max_rows")
        max_stored = sem("max_stored")
        max_chain = sem("max_chain")

        block = ctx.enter_context(nc.Block())

        def s_tile(u):
            return ps[:, 2 * (u % 3):2 * (u % 3) + 2, :]

        @block.sync
        def _(sp):
            sp.dma_start(wq[:], w_qkv).then_inc(in_w, 16)
            for t in range(2):
                sp.dma_start(xT[:, t * CH:(t + 1) * CH], x_t[:, t * CH:(t + 1) * CH]).then_inc(in_x[t], 16)
            sp.dma_start(col[:, 0:NCOL], cols).then_inc(in_small, 16)
            sp.dma_start(mean8[:], means).then_inc(in_small, 16)
            sp.dma_start(srow[:], scale_rows).then_inc(in_small, 16)
            sp.dma_start(cosT, cosines).then_inc(in_rope, 16)
            sp.dma_start(sinT, sines).then_inc(in_rope, 16)
            for t in range(2, NCH):
                sp.dma_start(xT[:, t * CH:(t + 1) * CH], x_t[:, t * CH:(t + 1) * CH]).then_inc(in_x[t], 16)
            sp.dma_start(ident[:], eye).then_inc(in_res, 16)
            sp.dma_start(bias_b[:], bias).then_inc(in_res, 16)
            sp.dma_start(wp[:], w_proj).then_inc(in_res, 16)
            sp.dma_start(xb[:], x_n.rearrange("(t p) c -> p t c", p=P)).then_inc(in_res, 16)
            for src, at in ((w1, W1), (w2, W2), (w3, W3)):
                if at == W3:
                    sp.dma_start(w_raw[:, at:at + HM * P].rearrange("p (k o) -> p k o", k=HM),
                                 src.rearrange("(k p) o -> p k o", p=P)).then_inc(in_ffn, 16)
                else:
                    sp.dma_start(w_raw[:, at:at + HID], src).then_inc(in_ffn, 16)
            for src, at in ((h1, H1), (h2, H2)):
                sp.dma_start(w_raw[:, at:at + HM * HID].rearrange("p (k o) -> p k o", k=HM),
                             src.rearrange("(k p) o -> p k o", p=P)).then_inc(in_ffn, 16)
            sp.wait_ge(zeros_set, 1)
            for c in range(NCH):
                sp.dma_start(m_scr.rearrange("a h t -> (a h) t")[:, c * CH:(c + 1) * CH], zero16[:]).then_inc(shift_zero, 16)

            def store_parts(t):
                sp.wait_ge(p3_done, t + 1)
                for i in range(5):
                    sp.dma_start(q_scr[:, i * HD:(i + 1) * HD, t * CH:(t + 1) * CH],
                                 parts[:, t % 2, i % PARTS, 0:CH]).then_inc(scr_out[t % 2], 16)
                for i in range(PARTS):
                    sp.dma_start(k_scr[:, i * HD:(i + 1) * HD, t * CH:(t + 1) * CH],
                                 parts[:, t % 2, i, CH:2 * CH]).then_inc(scr_out[t % 2], 16)

            def load_group(c, g, first=False):
                slot = g % 2
                if not first:
                    sp.wait_ge(pv_done, (4 * c + g - 1) * KT)
                b = c // 2
                for s in range(PARTS):
                    sp.dma_start(ka[24 * s:24 * s + 24, slot],
                                 k_scr[HG * g:HG * g + HG, :, bass.ds(b * SEQ, SEQ)].rearrange("h r t -> r h t")).then_inc(aug_in[slot], 16)
                    sp.dma_start(qa[24 * s:24 * s + 24, slot],
                                 q_scr[HG * g:HG * g + HG, HD * s:HD * s + 24, bass.ds(c * CH, CH)].rearrange("h r t -> r h t")).then_inc(aug_in[slot], 16)
                sp.dma_start(qa[MROW:MROW + PARTS, slot],
                             m_scr[:, HG * g:HG * g + HG, bass.ds(c * CH, CH)]).then_inc(aug_in[slot], 16)
                vw = KT * HG * VW
                sp.dma_start(va[:, slot].rearrange("p k h v -> p (k h v)"),
                             v_all[:].rearrange("p b g k h v -> p (b g k h v)")[:, bass.ds(b * NG * vw + g * vw, vw)]).then_inc(aug_in[slot], 16)

            def load_for_max(n, b, g):
                sp.wait_ge(max_split, n + 1)
                for s in range(PARTS):
                    sp.dma_start(ka[24 * s:24 * s + 24, 0],
                                 k_scr[bass.ds(HG * g, HG), 0:24, bass.ds(b * SEQ, SEQ)].rearrange("h r t -> r h t")).then_inc(max_in, 16)
                    for i in range(2):
                        sp.dma_start(qa[24 * s:24 * s + 24, i],
                                     q_scr[bass.ds(HG * g, HG), HD * s:HD * s + 24, bass.ds(b * SEQ + i * CH, CH)].rearrange("h r t -> r h t")).then_inc(max_in, 16)

            store_parts(0)
            store_parts(1)
            sp.wait_ge(v_ones, 1)
            sp.wait_ge(rows_set, 2)
            sp.wait_ge(shift_zero, 16 * NCH)
            sp.wait_ge(bound_flag, 1)
            wide = sp.value_load(flags_i[0:1, 0:1], min_val=0, max_val=1)
            with sp.If(wide == 1):
                store_parts(2)
                store_parts(3)
                sp.wait_ge(scr_out[0], 256)
                sp.wait_ge(scr_out[1], 256)
                with sp.Fori(0, BATCH) as b:
                    with sp.Fori(0, NG) as g:
                        n = NG * b + g
                        load_for_max(n, b, g)
                        sp.wait_ge(max_rows, n + 1)
                        for i in range(PARTS):
                            sp.dma_start(m_scr[i, bass.ds(HG * g, HG), bass.ds(b * SEQ, SEQ)],
                                         max_row[i * MT:(i + 1) * MT, :]).then_inc(max_stored, 16)
                sp.wait_ge(max_stored, 16 * PARTS * BATCH * NG)
            sp.wait_ge(v_evac, 2)
            sp.wait_ge(scr_out[0], 128)
            sp.wait_ge(scr_out[1], 128)
            load_group(0, 0, True)
            load_group(0, 1, True)
            with sp.If(wide == 0):
                store_parts(2)
                store_parts(3)
            load_group(0, 2)
            load_group(0, 3)
            sp.wait_ge(v_evac, 4)
            sp.wait_ge(scr_out[0], 256)
            sp.wait_ge(scr_out[1], 256)
            with sp.Fori(1, NCH) as c:
                for g in range(NG):
                    load_group(c, g)

        @block.gpsimd
        def _(pool):
            pool.memset(v_all[:], 1.0).then_inc(v_ones, 1)
            pool.memset(zero16[:].bitcast(F32), 0.0).then_inc(zeros_set, 1)
            pool.memset(mhalf[:], -0.5).then_inc(half_set, 1)
            two_ones = float(np.array([0x3F803F80], np.uint32).view(np.float32)[0])
            pool.wait_ge(v_ones, 1)
            pool.wait_ge(zeros_set, 1)
            pool.wait_ge(half_set, 1)
            pool.memset(ka[64:P].rearrange("p s h t -> p (s h t)").bitcast(F32), two_ones).then_inc(rows_set, 1)
            pool.memset(qa[64:P].rearrange("p s h t -> p (s h t)").bitcast(F32), 0.0).then_inc(rows_set, 1)
            pool.wait_ge(rows_set, 2)
            for t in range(NCH):
                pool.wait_ge(p2_done, t + 1)
                pool.tensor_tensor(parts[:, t % 2, 2, :], res, parts[:, t % 2, 1, :], ALU.subtract).then_inc(p3_done, 1)
            pool.wait_ge(in_res, 64)
            pool.tensor_tensor(xb[:], xb[:], bias_b[:, None, :].to_broadcast([P, NCH * TILES, P]), ALU.add).then_inc(res_add, 1)

            def rsqrt(n):
                pool.wait_ge(var1, n + 1)
                pool.tensor_tensor(rs[:], ve[:], mhalf[:], ALU.pow).then_inc(rstd, 1)

            def finish(c):
                rsqrt(2 * c)
                rsqrt(2 * c + 1)
                pool.wait_ge(y_ready, c + 1)
                pool.dma_start(out.rearrange("(t p) c -> p t c", p=P)[:, bass.ds(c * TILES, TILES), :], yo).then_inc(stored, 16)
                pool.wait_ge(stored, 16 * (c + 1))
                pool.nop().then_inc(yo_free, 1)

            pool.nop().then_inc(yo_free, 1)
            with pool.Fori(0, NCH) as c:
                finish(c)

        @block.tensor
        def _(pe):
            def prepare(t):
                pe.wait_ge(in_x[t], 16)
                wait(pe, rot_done, t)
                wait(pe, sq_done, t)
                for i in range(4):
                    mm = pe.matmul(ps[:, i, :], wq[:, i * P:(i + 1) * P], xT[:, t * CH:(t + 1) * CH], start=True, stop=True)
                mm.then_inc(qk_proj, 1)
                wait(pe, v_evac, t - 1)
                for i in range(TILES):
                    mm = pe.matmul(ps[:, 6 + t % 2, i * P:(i + 1) * P], xT[:, t * CH + i * P:t * CH + (i + 1) * P],
                                   wq[:, 4 * P:5 * P], start=True, stop=True)
                mm.then_inc(v_proj, 1)
                pe.wait_ge(sq_done, t + 1)
                wait(pe, ln_done, t)
                for i in range(2):
                    mm = pe.matmul(ps[:, 4 + i, :], mean8[:], sq[:, i * CH:(i + 1) * CH], start=True, stop=True)
                mm.then_inc(var_ready, 1)

            def logits(c, step, pair):
                g, kt = divmod(step, KT)
                slot = g % 2
                if kt == 0 and pair == 0:
                    pe.wait_ge(aug_in[slot], 128 * (2 * c + g // 2 + 1))
                u = 2 * step + pair
                wait(pe, exp_done, 64 * c + (u - 2 if u >= 3 else (0, -2, -1)[u]) if u >= 3 or not isinstance(c, int) else 0)
                for i in range(2):
                    h = 2 * pair + i
                    mm = pe.matmul(s_tile(u)[:, i, :], ka[:, slot, h, kt * P:(kt + 1) * P], qa[:, slot, h, :], start=True, stop=True)
                mm.then_inc(qk_ready, 1)

            def values(c, step):
                g, kt = divmod(step, KT)
                pe.wait_ge(exp_done, 64 * c + 2 * step + 2)
                if kt == 0:
                    wait(pe, o_copied, 4 * c + g)
                for h in range(HG):
                    mm = pe.matmul(ps[32 * h:32 * h + VW, O_BANK, :], va[:, g % 2, kt, h, :], probs[:, step % 4, h, :],
                                   start=(kt == 0), stop=(kt == KT - 1))
                mm.then_inc(pv_done, 1)

            use = [0, 0]

            def mix(base):
                n = use[1]
                use[1] += 1
                wait(pe, mix_free, base + n)
                return ps[:, MIX_BANK, :]

            def o_transpose(base, c, g):
                bank = mix(base)
                pe.wait_ge(o_copied, 4 * c + g + 1)
                for i in range(TILES):
                    mm = pe.transpose(bank[:, i * P:(i + 1) * P], oT[:, g % 2, i * P:(i + 1) * P], ident[:])
                mm.then_inc(mix_ready, 1)

            def project(base, c, stage):
                bank = mix(base)
                if stage == 0:
                    pe.wait_ge(attn_ready, 4 * c + 4)
                    for i in range(TILES):
                        mm = pe.transpose(bank[:, i * P:(i + 1) * P], attn[:, i, :], ident[:])
                else:
                    for i in range(TILES):
                        mm = pe.matmul(bank[:, i * P:(i + 1) * P], attnT[:, i * P:(i + 1) * P], wp[:], start=True, stop=True)
                mm.then_inc(mix_ready, 1)

            def x_transpose(base, c):
                bank = mix(base)
                pe.wait_ge(x1_ready, c + 1)
                for i in range(TILES):
                    mm = pe.transpose(bank[:, i * P:(i + 1) * P], x1[:, i, :], ident[:])
                mm.then_inc(mix_ready, 1)

            def w_at(col0):
                return w_hi[:, col0:col0 + P], w_lo[:, col0:col0 + P]

            def up(base, c, i, passes):
                m, w = i // 2, (W1, W2)[i % 2]
                bank = mix(base)
                pe.wait_ge(xs_ready, c + 1)
                todo = [(a, x) for a in w_at(w + m * P)[:1 + (passes > 2)] for x in (x_hi[:], x_lo[:])]
                for j, (a, x) in enumerate(todo):
                    mm = pe.matmul(bank, a, x, start=(j == 0), stop=(j == len(todo) - 1))
                mm.then_inc(mix_ready, 1)

            def from_tiles(bank, c, layer, w_of, first, passes):
                for k in range(HM):
                    if first:
                        pe.wait_ge(g_ready, 12 * c + HM * layer + k + 1)
                    todo = [(w, x) for w in w_at(w_of(k))[:1 + (passes > 2)] for x in (g_hi[:, k, :], g_lo[:, k, :])]
                    for i, (w, x) in enumerate(todo):
                        mm = pe.matmul(bank, w, x, start=(k == 0 and i == 0), stop=(k == HM - 1 and i == len(todo) - 1))
                mm.then_inc(mix_ready, 1)

            def hidden(base, c, layer, m, passes):
                from_tiles(mix(base), c, layer, lambda k: (H1, H2)[layer] + k * HID + m * P, m == 0, passes)

            def down(base, c, passes):
                from_tiles(mix(base), c, 2, lambda k: W3 + k * P, True, passes)

            def y_transpose(base, c):
                bank = mix(base)
                pe.wait_ge(yT_ready, c + 1)
                for i in range(TILES):
                    mm = pe.transpose(bank[:, i * P:(i + 1) * P], yT[:, i * P:(i + 1) * P], ident[:])
                mm.then_inc(mix_ready, 1)

            def ffn_at(base, c, slot, passes):
                if slot == 3:
                    o_transpose(base, c, NG - 1)
                if slot == 5:
                    project(base, c, 0)
                if slot == 7:
                    project(base, c, 1)
                if slot == X_SLOT:
                    x_transpose(base, c)
                if slot in UP_SLOTS:
                    up(base, c, UP_SLOTS.index(slot), passes)
                for layer in range(2):
                    if slot in HIDDEN_SLOTS[layer]:
                        hidden(base, c, layer, HIDDEN_SLOTS[layer].index(slot), passes)
                if slot == DOWN_SLOT:
                    down(base, c, passes)
                if slot == Y_SLOT:
                    y_transpose(base, c)

            def chunk(c, passes):
                base = 0 if passes == 0 else MIX_CHUNK * (c - 1) + MIX_FIRST
                use[1] = 0
                for step in range(STEPS):
                    logits(c, step, 0)
                    if passes:
                        ffn_at(base, c - 1, 2 * step, passes)
                    logits(c, step, 1)
                    if step:
                        values(c, step - 1)
                    elif passes:
                        values(c - 1, STEPS - 1)
                    if passes:
                        ffn_at(base, c - 1, 2 * step + 1, passes)
                    if 2 * step + 1 in O_SLOTS:
                        o_transpose(base, c, O_SLOTS.index(2 * step + 1))

            def last_layer(done, bank0, w, rows, cols, passes, inputs):
                for k in range(rows):
                    inputs(k)
                    for m in range(cols):
                        terms = [(a, x) for a in w_at(w + (k * HID if cols > 1 else k * P) + m * P)[:1 + (passes > 2)]
                                 for x in (g_hi[:, k, :], g_lo[:, k, :])]
                        for i, (a, x) in enumerate(terms):
                            mm = pe.matmul(ps[:, bank0 + m, :], a, x, start=(k == 0 and i == 0),
                                           stop=(k == rows - 1 and i == len(terms) - 1))
                        if k == rows - 1:
                            mm.then_inc(done, 1)

            def last_chunk(passes):
                base, c = MIX_CHUNK * (NCH - 1) + MIX_FIRST, NCH - 1
                use[1] = 0
                values(c, STEPS - 1)
                o_transpose(base, c, NG - 1)
                project(base, c, 0)
                project(base, c, 1)
                x_transpose(base, c)
                pe.wait_ge(xs_ready, c + 1)
                for m in range(HM):
                    for i, w in enumerate((W1, W2)):
                        terms = [(a, x) for a in w_at(w + m * P)[:1 + (passes > 2)] for x in (x_hi[:], x_lo[:])]
                        for j, (a, x) in enumerate(terms):
                            mm = pe.matmul(ps[:, 2 * m + i, :], a, x, start=(j == 0), stop=(j == len(terms) - 1))
                    mm.then_inc(last_up, 1)
                last_layer(last_hidden, 0, H1, HM, HM, passes, lambda k: pe.wait_ge(last_split, max(k, 1) + 1))
                last_layer(last_hidden, HM, H2, HM, HM, passes, lambda k: pe.wait_ge(last_split, HM + k + 1))
                last_layer(mix_ready, MIX_BANK - 7, W3, HM, 1, passes, lambda k: pe.wait_ge(last_split, 2 * HM + k + 1))
                pe.wait_ge(yT_ready, c + 1)
                for i in range(TILES):
                    mm = pe.transpose(ps[:, MIX_BANK, i * P:(i + 1) * P], yT[:, i * P:(i + 1) * P], ident[:])
                mm.then_inc(mix_ready, 1)

            def later_chunks(passes):
                with pe.Fori(1, NCH) as c:
                    chunk(c, passes)
                    assert use[1] == MIX_CHUNK
                last_chunk(passes)

            pe.wait_ge(warm_set, 1)
            for _ in range(WARM):
                pe.matmul(ps[:, MIX_BANK, :], warm[:, 0:P], warm[:], start=True, stop=True)
            pe.wait_ge(in_w, 16)
            pe.wait_ge(in_small, 48)
            for t in range(NCH):
                prepare(t)
            pe.wait_ge(rot_done, NCH)
            pe.wait_ge(ln_done, NCH)
            pe.wait_ge(v_evac, NCH)
            pe.wait_ge(o_rows_set, 1)
            pe.wait_ge(in_res, 64)

            def row_maxima(n):
                pe.wait_ge(max_in, 144 * (n + 1))
                for u in range(MT):
                    h, t = divmod(u, KT)
                    if u >= 3:
                        pe.wait_ge(max_taken, MT * n + u - 2)
                    for i in range(2):
                        mm = pe.matmul(s_tile(u)[:, i, :], qa[:, t // TILES, h, (t % TILES) * P:(t % TILES + 1) * P],
                                       ka[:, 0, h, i * CH:(i + 1) * CH], start=True, stop=True)
                    mm.then_inc(max_logits, 1)
                pe.wait_ge(max_split, n + 2)
                pe.transpose(ps[0:PARTS * MT, MIX_BANK, 0:P], max_parts, ident[:]).then_inc(max_turned, 1)

            pe.wait_ge(bound_flag, 1)
            wide = pe.value_load(flags_i[0:1, 0:1], min_val=0, max_val=1)
            with pe.If(wide == 1):
                with pe.Fori(0, BATCH * NG) as n:
                    row_maxima(n)
                pe.wait_ge(max_rows, BATCH * NG)

            chunk(0, 0)
            bank = mix(0)
            pe.wait_ge(w_split, 1)
            pe.matmul(bank[0:1, 0:1], ve[:, 0:1], ones_c[:], start=True, stop=True).then_inc(mix_ready, 1)
            pe.wait_ge(lo_flag, 1)
            low = pe.value_load(flags_i[0:1, 1:2], min_val=0, max_val=1)
            with pe.If(low == 0):
                later_chunks(2)
            with pe.If(low == 1):
                later_chunks(4)

        @block.scalar
        def _(act):
            act.preload_act_table_set("natural_log_exp_and_others")
            act.wait_ge(consts, 1)

            def part(i, t):
                if i == 0:
                    act.wait_ge(h_done, t + 1)
                    if t >= 2:
                        act.wait_ge(scr_out[t % 2], 128)
                    nc.scalar.copy(parts[:, t % 2, 0, :], hn).then_inc(p1_done, 1)
                else:
                    act.wait_ge(res_done, t + 1)
                    nc.scalar.copy(parts[:, t % 2, 1, :], res).then_inc(p2_done, 1)

            for t in range(NCH):
                act.wait_ge(qk_proj, t + 1)
                wait(act, var_ready, t)
                nc.scalar.activation(sq, ps[:, 0:2, :].rearrange("p a q -> p (a q)"), ACT.Square).then_inc(sq_done, 1)
                if t:
                    part(0, t - 1)
                act.wait_ge(var_ready, t + 1)
                wait(act, rinv_done, t)
                nc.scalar.activation(lnv, ps[:, 4:6, :].rearrange("p a q -> p (a q)"), ACT.Ln, bias=eps_c[:]).then_inc(ln_done, 1)
                act.wait_ge(ln_done, t + 1)
                wait(act, h_done, t)
                nc.scalar.activation(rinv, lnv, ACT.Exp, scale=-0.5).then_inc(rinv_done, 1)
                if t:
                    part(1, t - 1)
                act.wait_ge(v_proj, t + 1)
                if t == 0:
                    act.wait_ge(v_ones, 1)
                for i in range(TILES):
                    kt = (t % 2) * TILES + i
                    ins = nc.scalar.copy(v_all[:, t // 2, :, kt, :, 0:HD],
                                         ps[:, 6 + t % 2, i * P:(i + 1) * P].rearrange("p (g h d) -> p g h d", g=NG, h=HG))
                ins.then_inc(v_evac, 1)
            part(0, NCH - 1)
            part(1, NCH - 1)
            act.preload_act_table_set("exp_and_others")

            act.wait_ge(p3_done, NCH)

            def exps(c, step):
                for pair in range(2):
                    u = 2 * step + pair
                    act.wait_ge(qk_ready, 64 * c + u + 1)
                    if pair == 0:
                        wait(act, pv_done, 32 * c + step - 3)
                    nc.scalar.activation(probs[:, step % 4, 2 * pair:2 * pair + 2, :], s_tile(u), ACT.Exp).then_inc(exp_done, 1)

            def gate(c, m):
                act.wait_ge(pre_ready, 8 * c + m + 1)
                nc.scalar.activation(act_o[:, m * CH:(m + 1) * CH], pre_a[:, m * CH:(m + 1) * CH], ACT.Tanh, scale=0.5).then_inc(act_done, 1)

            def gelu(c, layer):
                for i, tiles in enumerate((slice(0, (HM - 1) * CH), slice((HM - 1) * CH, HM * CH))):
                    act.wait_ge(pre_ready, 8 * c + HM + 2 * layer + i + 1)
                    nc.scalar.activation(act_o[:, tiles], pre_a[:, tiles], ACT.Gelu).then_inc(act_done, 1)

            for step in range(STEPS):
                exps(0, step)
            with act.Fori(1, NCH) as c:
                for step in range(STEPS):
                    exps(c, step)
                    if step in GATE_STEPS:
                        gate(c - 1, GATE_STEPS.index(step))
                    if step in GELU_STEPS:
                        gelu(c - 1, GELU_STEPS.index(step))

            act.preload_act_table(ACT.Silu)
            for m in range(HM):
                act.wait_ge(last_up, m + 1)
                nc.scalar.activation(act_o[:, m * CH:(m + 1) * CH], ps[:, 2 * m, :], ACT.Silu, scale=col[:, C_S1 + m:C_S1 + m + 1]).then_inc(last_act, 1)
            act.preload_act_table(ACT.Gelu)
            for layer in range(2):
                for m in range(HM):
                    act.wait_ge(last_hidden, HM * layer + m + 1)
                    act.wait_ge(last_split, HM * layer + m + 1)
                    nc.scalar.activation(act_o[:, m * CH:(m + 1) * CH], ps[:, HM * layer + m, :], ACT.Gelu,
                                         scale=col[:, (C_H1, C_H2)[layer] + m:(C_H1, C_H2)[layer] + m + 1]).then_inc(last_act, 1)

        @block.vector
        def _(dve):
            links = [0]

            def link(ins, base):
                links[0] += 1
                ins.then_inc(chain, 1)
                dve.wait_ge(chain, base + links[0])

            nc.vector.memset(warm[:], 0.0).then_inc(warm_set, 1)
            nc.vector.memset(eps_c[:], EPS_RMS)
            nc.vector.memset(ones_c[:], 1.0).then_inc(consts, 1)
            dve.wait_ge(in_small, 48)
            for i in range(2):
                ins = nc.vector.tensor_reduce(flags[:, i:i + 1], srow[:, i * HD:(i + 1) * HD], AX.X, ALU.max, apply_absolute_value=True)
            link(ins, 0)
            link(nc.vector.tensor_scalar(flags[:, 2:3], flags[:, 0:1], flags[:, 1:2], HD ** 0.5, ALU.mult, ALU.mult), 0)
            link(nc.vector.tensor_scalar(flags[:, 3:4], flags[:, 2:3], LOGIT_BOUND, None, ALU.is_gt), 0)
            nc.vector.tensor_copy(flags_i[:, 0:1], flags[:, 3:4]).then_inc(bound_flag, 1)
            link(nc.vector.tensor_scalar(col[:, C_Q:C_QS + 1], col[:, C_Q:C_QS + 1], HD ** -0.5, None, ALU.mult), 0)
            nc.vector.tensor_scalar(col[:, C_S2H:C_S2H + HM], col[:, C_S2:C_S2 + HM], 0.5, None, ALU.mult)
            dve.wait_ge(in_rope, 32)

            def residue(t):
                dve.wait_ge(p1_done, t + 1)
                dve.wait_ge(h_done, t + 1)
                wait(dve, p3_done, t)
                nc.vector.tensor_tensor(res, hn, parts[:, t % 2, 0, :], ALU.subtract).then_inc(res_done, 1)

            for t in range(NCH):
                half = (t % 2) * CH
                dve.wait_ge(qk_proj, t + 1)
                for i, c_, table, dst in ((2, C_QS, sinT, rot_b), (3, C_KS, sinT, rot_b), (0, C_Q, cosT, rot_a), (1, C_K, cosT, rot_a)):
                    if i == 0:
                        dve.wait_ge(sq_done, t + 1)
                        wait(dve, h_done, t)
                    ins = nc.vector.scalar_tensor_tensor(
                        out=dst[:, (i % 2) * CH:(i % 2 + 1) * CH], in0=ps[:, i, :], scalar=col[:, c_:c_ + 1],
                        in1=table[:, half:half + CH], op0=ALU.mult, op1=ALU.mult)
                ins.then_inc(rot_done, 1)
                dve.wait_ge(rot_done, t + 1)
                link(nc.vector.tensor_tensor(rot_a, rot_a, rot_b, ALU.add), 0)
                if t:
                    residue(t - 1)
                    dve.wait_ge(res_done, t)
                dve.wait_ge(rinv_done, t + 1)
                nc.vector.tensor_tensor(hn, rot_a, rinv, ALU.mult).then_inc(h_done, 1)
            residue(NCH - 1)
            dve.wait_ge(v_evac, NCH)
            nc.vector.memset(ps[:, O_BANK, :], 0.0).then_inc(o_rows_set, 1)

            use = [0]

            def mixed(base):
                n = use[0]
                use[0] += 1
                dve.wait_ge(mix_ready, base + n + 1)
                return n

            mix_bank = ps[:, MIX_BANK, :]

            def copy_o(c, g):
                dve.wait_ge(pv_done, KT * (4 * c + g + 1))
                nc.vector.tensor_copy(oT[:, g % 2, :], ps[:, O_BANK, :]).then_inc(o_copied, 1)

            def normalise(base, cb, g):
                n = mixed(base)
                bank = mix_bank.rearrange("p (t h r) -> p t h r", t=TILES, h=HG)
                link(nc.vector.reciprocal(rden[:], bank[:, :, :, HD]), cb)
                dst = attn[:, :, g * 32:(g + 1) * 32].rearrange("p t (h d) -> p t h d", h=HG)
                nc.vector.tensor_tensor(dst, bank[:, :, :, 0:HD], rden[:, :, :, None].to_broadcast([P, TILES, HG, HD]),
                                        ALU.mult).then_inc(mix_free, 1)
                dve.wait_ge(mix_free, base + n + 1)
                dve.nop().then_inc(attn_ready, 1)

            def layer_norm(cb, src):
                for i in range(TILES):
                    ins = nc.vector.bn_stats(stats[:, i, :], src[:, i, :])
                link(ins, cb)
                nc.vector.memset(ve[:], 0.0)
                for i in range(TILES):
                    ins = nc.vector.bn_aggr(mv[:, i, :], stats[:, i, :])
                link(ins, cb)
                nc.vector.tensor_scalar(ve[:], mv[:, :, 1], EPS_LN, None, ALU.add).then_inc(var1, 1)

            def scale_rows_of(n, src, dst):
                dve.wait_ge(rstd, n)
                for i in range(TILES):
                    ins = nc.vector.tensor_scalar(dst[:, i, :], src[:, i, :], mv[:, i, 0:1], rs[:, i:i + 1],
                                                  ALU.subtract, ALU.mult)
                return ins

            def split(cb, src, hi, lo):
                link(nc.vector.tensor_copy(hi, src), cb)
                return nc.vector.tensor_tensor(lo, src, hi.bitcast(F32), ALU.subtract)

            def residual(base, cb, c, tail=False):
                n = mixed(base)
                xr = xb[:].rearrange("p t c -> p (t c)")[:, bass.ds(c * CH, CH)]
                nc.vector.tensor_tensor(r1[:].rearrange("p t c -> p (t c)"), mix_bank, xr, ALU.add).then_inc(mix_free, 1)
                dve.wait_ge(mix_free, base + n + 1)
                layer_norm(cb, r1)
                scale_rows_of(2 * c + 1, r1, x1).then_inc(x1_ready, 1)

            def split_x(base, cb):
                n = mixed(base)
                split(cb, mix_bank, x_hi[:], x_lo[:]).then_inc(mix_free, 1)
                dve.wait_ge(mix_free, base + n + 1)
                dve.nop().then_inc(xs_ready, 1)

            def copy_attention(base):
                mixed(base)
                nc.vector.tensor_copy(attnT, mix_bank).then_inc(mix_free, 1)

            def pre_activation(base, m, c0, signal, gated=False):
                n = mixed(base)
                a, b = (v[:, m * CH:(m + 1) * CH] for v in (pre_a, pre_b))
                if gated:
                    ins = nc.vector.scalar_tensor_tensor(out=b, in0=mix_bank, scalar=col[:, c0 + m:c0 + m + 1], in1=a,
                                                         op0=ALU.mult, op1=ALU.mult)
                else:
                    ins = nc.vector.tensor_scalar(a, mix_bank, col[:, c0 + m:c0 + m + 1], None, ALU.mult)
                ins.then_inc(mix_free, 1)
                if signal:
                    dve.wait_ge(mix_free, base + n + 1)
                    dve.nop().then_inc(pre_ready, 1)

            def split_tile(cb, m):
                cols_m = act_o[:, m * CH:(m + 1) * CH]
                return split(cb, cols_m, g_hi[:, m, :], g_lo[:, m, :])

            def gate(cb, c, m):
                a, b = (v[:, m * CH:(m + 1) * CH] for v in (act_o, pre_b))
                dve.wait_ge(act_done, 8 * c + m + 1)
                link(nc.vector.scalar_tensor_tensor(out=a, in0=a, scalar=1.0, in1=b, op0=ALU.add, op1=ALU.mult), cb)
                split_tile(cb, m).then_inc(g_ready, 1)

            def gelu_split(cb, c, layer):
                for m in range(HM):
                    if m in (0, HM - 1):
                        dve.wait_ge(act_done, 8 * c + HM + 2 * layer + (1 if m == 0 else 2))
                    split_tile(cb, m).then_inc(g_ready, 1)

            def scale_y(base, c, bank):
                n = mixed(base)
                nc.vector.tensor_scalar(yT, bank, col[:, C_W3:C_W3 + 1], None, ALU.mult).then_inc(mix_free, 1)
                dve.wait_ge(mix_free, base + n + 1)
                dve.nop().then_inc(yT_ready, 1)

            def finish(base, cb, c):
                n = mixed(base)
                nc.vector.tensor_tensor(r1[:].rearrange("p t c -> p (t c)"), mix_bank,
                                        x1.rearrange("p t c -> p (t c)"), ALU.add).then_inc(mix_free, 1)
                dve.wait_ge(mix_free, base + n + 1)
                layer_norm(cb, r1)
                dve.wait_ge(yo_free, c + 1)
                scale_rows_of(2 * c + 2, r1, yo).then_inc(y_ready, 1)

            def ffn_at(base, cb, c, slot):
                if slot == 3:
                    normalise(base, cb, NG - 1)
                if slot == 5:
                    copy_attention(base)
                if slot == 7:
                    residual(base, cb, c)
                if slot == X_SLOT:
                    split_x(base, cb)
                if slot in UP_SLOTS:
                    i = UP_SLOTS.index(slot)
                    pre_activation(base, i // 2, (C_S1, C_S2H)[i % 2], i % 2 == 1, gated=i % 2 == 1)
                if slot in GATE_SLOTS:
                    gate(cb, c, GATE_SLOTS.index(slot))
                for layer in range(2):
                    if slot in HIDDEN_SLOTS[layer]:
                        m = HIDDEN_SLOTS[layer].index(slot)
                        pre_activation(base, m, (C_H1, C_H2)[layer], m >= HM - 2)
                    if slot == SPLIT_SLOTS[layer]:
                        gelu_split(cb, c, layer)
                if slot == DOWN_SLOT:
                    scale_y(base, c, mix_bank)
                if slot == Y_SLOT:
                    finish(base, cb, c)

            def chunk(c, base, cb, with_ffn):
                for step in range(STEPS):
                    g, kt = divmod(step, KT)
                    if with_ffn:
                        ffn_at(base, cb, c - 1, 2 * step)
                    if kt == 0 and g:
                        copy_o(c, g - 1)
                    if kt == 0 and g == 0 and with_ffn:
                        copy_o(c - 1, NG - 1)
                    if with_ffn:
                        ffn_at(base, cb, c - 1, 2 * step + 1)
                    if 2 * step + 1 in O_SLOTS:
                        normalise(base, cb, O_SLOTS.index(2 * step + 1))

            def max_link(ins, n, k):
                ins.then_inc(max_chain, 1)
                dve.wait_ge(max_chain, 5 * n + k)

            def row_maxima(n):
                for u in range(MT):
                    dve.wait_ge(max_logits, MT * n + u + 1)
                    ins = nc.vector.tensor_reduce(neg_max[:, u:u + 1], s_tile(u).rearrange("p a q -> p (a q)"), AX.X, ALU.max, negate=True)
                    ins.then_inc(max_taken, 1)
                dve.wait_ge(max_taken, MT * (n + 1))
                src = neg_max
                for i in range(PARTS):
                    max_link(nc.vector.tensor_copy(part16, src), n, 2 * i + 1)
                    if i < PARTS - 1:
                        nc.vector.tensor_copy(max_parts[:, i * MT:(i + 1) * MT], part16)
                        max_link(nc.vector.tensor_tensor(max_res, src, part16, ALU.subtract), n, 2 * i + 2)
                    else:
                        nc.vector.tensor_copy(max_parts[:, i * MT:(i + 1) * MT], part16).then_inc(max_split, 1)
                    src = max_res
                dve.wait_ge(max_turned, n + 1)
                nc.vector.tensor_copy(max_row, ps[0:PARTS * MT, MIX_BANK, 0:P]).then_inc(max_rows, 1)
                dve.wait_ge(max_stored, 16 * PARTS * (n + 1))

            wide = dve.value_load(flags_i[0:1, 0:1], min_val=0, max_val=1)
            with dve.If(wide == 1):
                dve.nop().then_inc(max_split, 1)
                with dve.Fori(0, BATCH * NG) as n:
                    row_maxima(n)

            dve.wait_ge(in_ffn, 80)
            link(nc.vector.tensor_copy(w_hi[:], w_raw), 0)
            link(nc.vector.tensor_tensor(w_lo[:], w_raw, w_hi[:].bitcast(F32), ALU.subtract), 0)
            nc.vector.tensor_reduce(ve[:, 0:1], w_lo[:].bitcast(F32), AX.X, ALU.max, apply_absolute_value=True).then_inc(w_split, 1)
            chunk(0, 0, 0, False)
            n = mixed(0)
            link(nc.vector.tensor_scalar(flags[:, 0:1], mix_bank[0:1, 0:1], 0.0, None, ALU.not_equal), 0)
            nc.vector.tensor_copy(flags_i[:, 1:2], flags[:, 0:1]).then_inc(lo_flag, 1)
            dve.nop().then_inc(mix_free, 1)
            dve.wait_ge(res_add, 1)
            start = links[0]
            with dve.Fori(1, NCH) as c:
                use[0], links[0] = 0, 0
                chunk(c, MIX_CHUNK * (c - 1) + MIX_FIRST, CHAIN_CHUNK * (c - 1) + start, True)
                assert use[0] == MIX_CHUNK and links[0] == CHAIN_CHUNK, links[0]

            use[0], links[0] = 0, 0
            c, base, cb = NCH - 1, MIX_CHUNK * (NCH - 1) + MIX_FIRST, CHAIN_CHUNK * (NCH - 1) + start
            copy_o(c, NG - 1)
            normalise(base, cb, NG - 1)
            copy_attention(base)
            residual(base, cb, c)
            split_x(base, cb)
            for m in range(HM):
                a = act_o[:, m * CH:(m + 1) * CH]
                dve.wait_ge(last_act, m + 1)
                link(nc.vector.scalar_tensor_tensor(out=a, in0=ps[:, 2 * m + 1, :], scalar=col[:, C_S2 + m:C_S2 + m + 1],
                                                    in1=a, op0=ALU.mult, op1=ALU.mult), cb)
                split_tile(cb, m).then_inc(last_split, 1)
            for layer in range(2):
                for m in range(HM):
                    dve.wait_ge(last_act, HM * (layer + 1) + m + 1)
                    split_tile(cb, m).then_inc(last_split, 1)
            scale_y(base, c, ps[:, 0, :])
            finish(base, cb, c)


def kernel(**inputs):
    import concourse.bacc as bacc
    from concourse.bass_utils import run_bass_kernel_spmd

    a = {k.split("_", 1)[1]: np.ascontiguousarray(v) for k, v in inputs.items()}
    x = a["attn_x"].reshape(TOK, DIM)
    swap = (np.arange(DIM) // HD) * HD + (np.arange(DIM) + HD // 2) % HD
    w = a["attn_w_qkv"]
    w_q, w_k, w_v = w[:, :DIM], w[:, DIM:2 * DIM], w[:, 2 * DIM:]
    d_of = np.arange(DIM) % HD
    q_s, k_s = a["attn_q_scale"][d_of], a["attn_k_scale"][d_of]
    by_tile = lambda s: s.reshape(HM, P).T
    half = HD // 2
    freqs = (np.float32(1.0) / np.float32(1250) ** (np.arange(half, dtype=np.float32) / np.float32(half))).astype(np.float32)
    angle = np.outer(np.arange(SEQ, dtype=np.float32), freqs).astype(np.float32)[:, d_of % half].T
    sign = np.where(d_of < half, -1.0, 1.0).astype(np.float32)[:, None]
    same_head = np.arange(P)[:, None] // HD == np.arange(P)[None, :] // HD
    arrays = {
        "x_t": x.T, "x_n": x,
        "w_qkv": np.concatenate([w_q, w_k, w_q[:, swap], w_k[:, swap], w_v], axis=1),
        "cols": np.concatenate([by_tile(a["ffn_w1_s"]), by_tile(a["ffn_w2_s"]), by_tile(a["ffn_h1_s"]), by_tile(a["ffn_h2_s"]),
                                a["ffn_w3_s"][:, None], q_s[:, None], q_s[swap][:, None], k_s[:, None], k_s[swap][:, None]], axis=1),
        "scale_rows": np.concatenate([a["attn_q_scale"], a["attn_k_scale"]])[None, :],
        "bias": np.broadcast_to(a["attn_b_proj"][None, :], (P, DIM)),
        "w_proj": a["attn_w_proj"],
        "w1": a["ffn_w1_w"].T, "w2": a["ffn_w2_w"].T, "h1": a["ffn_h1_w"].T, "h2": a["ffn_h2_w"].T, "w3": a["ffn_w3_w"].T,
        "cosines": np.cos(angle).astype(np.float32), "sines": (np.sin(angle) * sign).astype(np.float32),
        "means": (same_head / HD).astype(np.float32), "eye": np.eye(P, dtype=np.float32),
    }
    nc = bacc.Bacc("TRN2", target_bir_lowering=False, num_devices=1)
    sent, args = {}, []
    for name, v in arrays.items():
        v = np.ascontiguousarray(v)
        sent[f"in_{name}"] = v
        args.append(nc.dram_tensor(f"in_{name}", v.shape, mybir.dt.from_np(v.dtype), kind="ExternalInput").ap())
    out = nc.dram_tensor("out_y", (TOK, DIM), F32, kind="ExternalOutput").ap()
    build(nc, *args, out)
    r = run_bass_kernel_spmd(nc, [sent], core_ids=[0])
    return r.results[0]["out_y"].reshape(BATCH, SEQ, DIM)
```

```python
from contextlib import ExitStack

import numpy as np

import concourse.bass as bass
from concourse import mybir

F32 = mybir.dt.float32
F32R = mybir.dt.float32r
BF16 = mybir.dt.bfloat16
I32 = mybir.dt.int32
ALU = mybir.AluOpType
ACT = mybir.ActivationFunctionType
AX = mybir.AxisListType

P = 128
BATCH, SEQ, DIM = 2, 1024, 128
HEADS, HD = 16, 8
TOK = BATCH * SEQ
HID = 512
CH = 512
NCH = TOK // CH
TILES = CH // P
HG = 4
NG = HEADS // HG
KT = SEQ // P
STEPS = NG * KT
PARTS = 3
QROWS = PARTS * PARTS * HD
MROW = QROWS
KROWS = P
HM = HID // P
VW = HD + 1
EPS_RMS, EPS_LN = 1e-6, 1e-5
LOGIT_BOUND = 60.0

MIX_FIRST = 4
MIX_CHUNK = 25
CHAIN_CHUNK = 25

C_S1, C_S2, C_H1, C_H2, C_W3 = 0, 4, 8, 12, 16
C_Q, C_QS, C_K, C_KS = 17, 18, 19, 20
NCOL = 21
C_S2H = NCOL
STORED = 16 * 6
LOADED = 16 * 4
KEEP_WARM = (14, 8)
WARM = 13
SLOTS = 2 * STEPS
UP_SLOTS = (16, 18, 22, 24, 25, 27, 29, 33)
GATE_STEPS = (10, 12, 14, 16)
GATE_SLOTS = (24, 28, 32, 36)
HIDDEN_SLOTS = ((36, 38, 40, 41), (46, 48, 50, 51))
GELU_STEPS = (20, 25)
GELU_TILES = ((0, 1, 2), (3,))
FLAG_SLOT = 40
SPLIT_SLOTS = (42, 52)
X_SLOT, DOWN_SLOT, Y_SLOT = 13, 56, 60
O_SLOTS = (19, 43, 53)


def wait(eng, sem, count):
    if isinstance(count, int) and count <= 0:
        return
    eng.wait_ge(sem, count)


def build(nc, x_t, x_n, w_qkv, cols, scale_rows, bias, w_proj, w1, w2, h1, h2, w3, cosines, sines, means, eye, out):
    ctx = ExitStack()
    with ctx:
        def sb(name, shape, dt):
            return ctx.enter_context(nc.sbuf_tensor(name, shape, dt))

        def sem(name):
            return ctx.enter_context(nc.semaphore(name))

        q_scr = nc.dram_tensor("q_scr", [HEADS * QROWS, TOK], BF16).ap()
        k_scr = nc.dram_tensor("k_scr", [HEADS * QROWS, TOK], BF16).ap()
        m_scr = nc.dram_tensor("m_scr", [PARTS, HEADS, TOK], BF16).ap()

        xT = sb("xT", [P, TOK], F32)
        xb = sb("xb", [P, NCH * TILES, P], F32)
        wq = sb("wq", [P, 5 * P], F32)
        col = sb("col", [P, NCOL + HM], F32)
        rope = sb("rope", [P, 4 * CH], F32)
        cosT, sinT = rope[:, 0:SEQ], rope[:, SEQ:2 * SEQ]
        attnT, yT = rope[:, 0:CH], rope[:, CH:2 * CH]
        x1, yo = (rope[:, i * CH:(i + 1) * CH].rearrange("p (t c) -> p t c", t=TILES) for i in (2, 3))
        mean8 = sb("mean8", [P, P], F32)
        ident = sb("ident", [P, P], F32)
        bias_b = sb("bias_b", [P, P], F32)
        wp = sb("wp", [P, P], F32)
        srow = sb("srow", [1, 2 * HD], F32)
        flags = sb("flags", [1, 4], F32)
        flags_i = sb("flags_i", [1, 2], I32)
        eps_c = sb("eps_c", [P, 1], F32)
        ones_c = sb("ones_c", [P, 1], F32)
        mhalf = sb("mhalf", [P, TILES], F32)
        warm = sb("warm", [P, CH], BF16)
        zero16 = sb("zero16", [PARTS * HEADS, CH], BF16)

        ka = sb("ka", [KROWS, 2, HG, SEQ], BF16)
        qa = sb("qa", [KROWS, 2, HG, CH], BF16)
        va = sb("va", [P, 2, KT, HG, VW], F32)
        v_all = sb("v_all", [P, BATCH, NG, KT, HG, VW], F32)
        probs = sb("probs", [P, 4, HG, CH], F32)
        parts = sb("parts", [P, 2, PARTS, 2 * CH], BF16)

        oT = sb("oT", [P, 2, CH], F32)
        rden = sb("rden", [P, TILES, HG], F32)
        attn = sb("attn", [P, TILES, P], F32)
        r1 = sb("r1", [P, TILES, P], F32)
        stats = sb("stats", [P, TILES, 6], F32)
        mv = sb("mv", [P, TILES, 2], F32)
        ve = sb("ve", [P, TILES], F32)
        rs = sb("rs", [P, TILES], F32)

        NW = 2 * HID + 2 * HM * HID + HM * P
        W1, W2, H1, H2, W3 = 0, HID, 2 * HID, 2 * HID + HM * HID, 2 * HID + 2 * HM * HID
        ffn = sb("ffn", [P, 3 * HM * CH], F32)
        w_raw = ffn[:, 0:NW]
        pre_a = ffn[:, 0:HM * CH]
        pre_b = ffn[:, HM * CH:2 * HM * CH]
        act_o = ffn[:, 2 * HM * CH:3 * HM * CH]
        w_hi = sb("w_hi", [P, NW], F32R)
        w_lo = sb("w_lo", [P, NW], F32R)
        x_hi = sb("x_hi", [P, CH], F32R)
        x_lo = sb("x_lo", [P, CH], F32R)
        g_hi = sb("g_hi", [P, HM, CH], F32R)
        g_lo = sb("g_lo", [P, HM, CH], F32R)

        prep = probs[:].rearrange("p a h q -> p (a h q)")
        W2K = 2 * CH
        sq, lnv, rinv, rot_a, rot_b, hn, res = (prep[:, i * W2K:(i + 1) * W2K] for i in range(7))

        MT = HG * KT
        a_flat = attn[:].rearrange("p t c -> p (t c)")
        neg_max, max_res, max_parts = a_flat[:, 0:MT], a_flat[:, MT:2 * MT], a_flat[:, 2 * MT:5 * MT]
        max_row = oT[0:PARTS * MT, 0, 0:P // 2].bitcast(BF16)
        part16 = oT[:, 1, 0:MT // 2].bitcast(BF16)

        ps = ctx.enter_context(nc.psum_tensor("ps", [P, 8, CH], F32))
        O_BANK, MIX_BANK = 6, 7

        in_w = sem("in_w")
        in_x = [sem(f"in_x{t}") for t in range(NCH)]
        in_rope = sem("in_rope")
        in_small = sem("in_small")
        in_res = sem("in_res")
        in_ffn = sem("in_ffn")
        zeros_set = sem("zeros_set")
        consts = sem("consts")
        v_ones = sem("v_ones")
        rows_set = sem("rows_set")
        half_set = sem("half_set")
        o_rows_set = sem("o_rows_set")
        warm_set = sem("warm_set")
        shift_zero = sem("shift_zero")
        qk_proj = sem("qk_proj")
        v_proj = sem("v_proj")
        sq_done = sem("sq_done")
        var_ready = sem("var_ready")
        ln_done = sem("ln_done")
        rinv_done = sem("rinv_done")
        rot_done = sem("rot_done")
        h_done = sem("h_done")
        p1_done = sem("p1_done")
        res_done = sem("res_done")
        p2_done = sem("p2_done")
        p3_done = sem("p3_done")
        v_evac = sem("v_evac")
        scr_out = [sem("scr_out0"), sem("scr_out1")]
        aug_in = [sem("aug_in0"), sem("aug_in1")]
        qk_ready = sem("qk_ready")
        exp_done = sem("exp_done")
        pv_done = sem("pv_done")
        o_copied = sem("o_copied")
        mix_ready = sem("mix_ready")
        mix_free = sem("mix_free")
        attn_ready = sem("attn_ready")
        var1 = sem("var_eps_ready")
        rstd = sem("rstd_ready")
        x1_ready = sem("x1_ready")
        xs_ready = sem("x_split_ready")
        pre_ready = sem("pre_ready")
        act_done = sem("act_done")
        g_ready = sem("g_split_ready")
        yT_ready = sem("yT_ready")
        y_ready = sem("y_ready")
        stored = sem("stored")
        yo_free = sem("yo_free")
        w_split = sem("w_split")
        lo_flag = sem("lo_flag")
        res_add = sem("res_add")
        chain = sem("chain")
        last_ready = sem("last_ready")
        last_given = sem("last_given")
        last_var = sem("last_var")
        last_rstd = sem("last_rstd")
        last_y = sem("last_y")
        last_stored = sem("last_stored")
        last_up = sem("last_up")
        last_read = sem("last_read")
        last_high = sem("last_high")
        last_hidden = sem("last_hidden")
        last_act = sem("last_act")
        last_split = sem("last_split")
        bound_flag = sem("bound_flag")
        max_in = sem("max_in")
        max_logits = sem("max_logits")
        max_taken = sem("max_taken")
        max_split = sem("max_split")
        max_turned = sem("max_turned")
        max_rows = sem("max_rows")
        max_stored = sem("max_stored")
        max_chain = sem("max_chain")

        block = ctx.enter_context(nc.Block())

        R_O, R_ATTN, R_PROJ, R_X, R_DOWN, R_Y = 0, 2, 4, 6, 8, 9
        G_O, G_ATTN, G_ATTN_T, G_X, G_SPLIT, G_Y = 0, 2, 4, 6, 8, 10
        HT = TILES // 2
        HC = CH // 2

        def s_tile(u):
            return ps[:, 2 * (u % 3):2 * (u % 3) + 2, :]

        @block.sync
        def _(sp):
            sp.dma_start(wq[:], w_qkv).then_inc(in_w, 16)
            for t in range(2):
                sp.dma_start(xT[:, t * CH:(t + 1) * CH], x_t[:, t * CH:(t + 1) * CH]).then_inc(in_x[t], 16)
            sp.dma_start(col[:, 0:NCOL], cols).then_inc(in_small, 16)
            sp.dma_start(mean8[:], means).then_inc(in_small, 16)
            sp.dma_start(srow[:], scale_rows).then_inc(in_small, 16)
            sp.dma_start(cosT, cosines).then_inc(in_rope, 16)
            sp.dma_start(sinT, sines).then_inc(in_rope, 16)
            for t in range(2, NCH):
                sp.dma_start(xT[:, t * CH:(t + 1) * CH], x_t[:, t * CH:(t + 1) * CH]).then_inc(in_x[t], 16)
            sp.dma_start(ident[:], eye).then_inc(in_res, 16)
            sp.dma_start(bias_b[:], bias).then_inc(in_res, 16)
            sp.dma_start(wp[:], w_proj).then_inc(in_res, 16)
            sp.dma_start(xb[:], x_n.rearrange("(t p) c -> p t c", p=P)).then_inc(in_res, 16)
            for src, at in ((w1, W1), (w2, W2), (w3, W3)):
                if at == W3:
                    sp.dma_start(w_raw[:, at:at + HM * P].rearrange("p (k o) -> p k o", k=HM),
                                 src.rearrange("(k p) o -> p k o", p=P)).then_inc(in_ffn, 16)
                else:
                    sp.dma_start(w_raw[:, at:at + HID], src).then_inc(in_ffn, 16)
            for src, at in ((h1, H1), (h2, H2)):
                sp.dma_start(w_raw[:, at:at + HM * HID].rearrange("p (k o) -> p k o", k=HM),
                             src.rearrange("(k p) o -> p k o", p=P)).then_inc(in_ffn, 16)
            sp.wait_ge(zeros_set, 1)
            for c in range(NCH):
                sp.dma_start(m_scr.rearrange("a h t -> (a h) t")[:, c * CH:(c + 1) * CH], zero16[:]).then_inc(shift_zero, 16)

            def store_parts(t):
                q_rows, k_rows = (v[:, t * CH:(t + 1) * CH].rearrange("(r b a) t -> r b a t", b=PARTS, a=PARTS) for v in (q_scr, k_scr))
                for i, done in enumerate((p1_done, p2_done, p3_done)):
                    sp.wait_ge(done, t + 1)
                    for rows, at in ((q_rows[:, :, i, :], 0), (k_rows[:, i, :, :], CH)):
                        sp.dma_start(rows, parts[:, t % 2, i:i + 1, at:at + CH].to_broadcast([P, PARTS, CH])).then_inc(scr_out[t % 2], 16)

            def load_rows(dst, scr, g, t0, count, signal):
                sp.dma_start(dst[0:QROWS], scr[bass.ds(HG * QROWS * g, HG * QROWS), bass.ds(t0, count)].rearrange("(h r) t -> r h t", h=HG)).then_inc(signal, 16)

            def load_group(c, g, first=False):
                slot = g % 2
                if not first:
                    sp.wait_ge(pv_done, (4 * c + g - 1) * KT)
                b = c // 2
                load_rows(ka[:, slot], k_scr, g, b * SEQ, SEQ, aug_in[slot])
                load_rows(qa[:, slot], q_scr, g, c * CH, CH, aug_in[slot])
                sp.dma_start(qa[MROW:MROW + PARTS, slot],
                             m_scr[:, HG * g:HG * g + HG, bass.ds(c * CH, CH)]).then_inc(aug_in[slot], 16)
                vw = KT * HG * VW
                sp.dma_start(va[:, slot].rearrange("p k h v -> p (k h v)"),
                             v_all[:].rearrange("p b g k h v -> p (b g k h v)")[:, bass.ds(b * NG * vw + g * vw, vw)]).then_inc(aug_in[slot], 16)

            def load_for_max(n, b, g):
                sp.wait_ge(max_split, n + 1)
                load_rows(ka[:, 0], k_scr, g, b * SEQ, SEQ, max_in)
                for i in range(2):
                    load_rows(qa[:, i], q_scr, g, b * SEQ + i * CH, CH, max_in)

            store_parts(0)
            store_parts(1)
            sp.wait_ge(v_ones, 1)
            sp.wait_ge(rows_set, 2)
            sp.wait_ge(shift_zero, 16 * NCH)
            sp.wait_ge(bound_flag, 1)
            wide = sp.value_load(flags_i[0:1, 0:1], min_val=0, max_val=1)
            with sp.If(wide == 1):
                store_parts(2)
                store_parts(3)
                sp.wait_ge(scr_out[0], 2 * STORED)
                sp.wait_ge(scr_out[1], 2 * STORED)
                with sp.Fori(0, BATCH) as b:
                    with sp.Fori(0, NG) as g:
                        n = NG * b + g
                        load_for_max(n, b, g)
                        sp.wait_ge(max_rows, n + 1)
                        for i in range(PARTS):
                            sp.dma_start(m_scr[i, bass.ds(HG * g, HG), bass.ds(b * SEQ, SEQ)],
                                         max_row[i * MT:(i + 1) * MT, :]).then_inc(max_stored, 16)
                sp.wait_ge(max_stored, 16 * PARTS * BATCH * NG)
            sp.wait_ge(v_evac, 2)
            sp.wait_ge(scr_out[0], STORED)
            sp.wait_ge(scr_out[1], STORED)
            load_group(0, 0, True)
            load_group(0, 1, True)
            with sp.If(wide == 0):
                store_parts(2)
                store_parts(3)
            load_group(0, 2)
            load_group(0, 3)
            sp.wait_ge(v_evac, 4)
            sp.wait_ge(scr_out[0], 2 * STORED)
            sp.wait_ge(scr_out[1], 2 * STORED)
            with sp.Fori(1, NCH) as c:
                for g in range(NG):
                    load_group(c, g)
            for hf in range(2):
                sp.wait_ge(last_y, hf + 1)
                t0 = (NCH - 1) * TILES + hf * HT
                sp.dma_start(out.rearrange("(t p) c -> p t c", p=P)[:, t0:t0 + HT, :], yo[:, hf * HT:(hf + 1) * HT, :]).then_inc(last_stored, 16)
            sp.wait_ge(last_stored, 32)

        @block.gpsimd
        def _(pool):
            pool.memset(v_all[:], 1.0).then_inc(v_ones, 1)
            pool.memset(zero16[:].bitcast(F32), 0.0).then_inc(zeros_set, 1)
            pool.memset(mhalf[:], -0.5).then_inc(half_set, 1)
            two_ones = float(np.array([0x3F803F80], np.uint32).view(np.float32)[0])
            pool.wait_ge(v_ones, 1)
            pool.wait_ge(zeros_set, 1)
            pool.wait_ge(half_set, 1)
            pool.memset(ka[64:P].rearrange("p s h t -> p (s h t)").bitcast(F32), two_ones).then_inc(rows_set, 1)
            pool.memset(qa[64:P].rearrange("p s h t -> p (s h t)").bitcast(F32), 0.0).then_inc(rows_set, 1)
            pool.wait_ge(rows_set, 2)
            for t in range(NCH):
                pool.wait_ge(p2_done, t + 1)
                pool.tensor_tensor(parts[:, t % 2, 2, :], res, parts[:, t % 2, 1, :], ALU.subtract).then_inc(p3_done, 1)
            pool.wait_ge(in_res, 64)
            pool.tensor_tensor(xb[:], xb[:], bias_b[:, None, :].to_broadcast([P, NCH * TILES, P]), ALU.add).then_inc(res_add, 1)

            def rsqrt(n):
                pool.wait_ge(var1, n + 1)
                pool.tensor_tensor(rs[:], ve[:], mhalf[:], ALU.pow).then_inc(rstd, 1)

            def finish(c):
                rsqrt(2 * c)
                rsqrt(2 * c + 1)
                pool.wait_ge(y_ready, c + 1)
                pool.dma_start(out.rearrange("(t p) c -> p t c", p=P)[:, bass.ds(c * TILES, TILES), :], yo).then_inc(stored, 16)
                pool.wait_ge(stored, 16 * (c + 1))
                pool.nop().then_inc(yo_free, 1)

            pool.nop().then_inc(yo_free, 1)
            with pool.Fori(0, NCH - 1) as c:
                finish(c)
            for n in range(4):
                tiles = slice((n % 2) * HT, (n % 2 + 1) * HT)
                pool.wait_ge(last_var, n + 1)
                pool.tensor_tensor(rs[:, tiles], ve[:, tiles], mhalf[:, tiles], ALU.pow).then_inc(last_rstd, 1)

        @block.tensor
        def _(pe):
            def prepare(t):
                pe.wait_ge(in_x[t], 16)
                wait(pe, rot_done, t)
                wait(pe, sq_done, t)
                for i in range(4):
                    mm = pe.matmul(ps[:, i, :], wq[:, i * P:(i + 1) * P], xT[:, t * CH:(t + 1) * CH], start=True, stop=True)
                mm.then_inc(qk_proj, 1)
                wait(pe, v_evac, t - 1)
                for i in range(TILES):
                    mm = pe.matmul(ps[:, 6 + t % 2, i * P:(i + 1) * P], xT[:, t * CH + i * P:t * CH + (i + 1) * P],
                                   wq[:, 4 * P:5 * P], start=True, stop=True)
                mm.then_inc(v_proj, 1)
                pe.wait_ge(sq_done, t + 1)
                wait(pe, ln_done, t)
                for i in range(2):
                    mm = pe.matmul(ps[:, 4 + i, :], mean8[:], sq[:, i * CH:(i + 1) * CH], start=True, stop=True)
                mm.then_inc(var_ready, 1)

            def logits(c, step, pair):
                g, kt = divmod(step, KT)
                slot = g % 2
                if kt == 0 and pair == 0:
                    pe.wait_ge(aug_in[slot], LOADED * (2 * c + g // 2 + 1))
                u = 2 * step + pair
                wait(pe, exp_done, 64 * c + (u - 2 if u >= 3 else (0, -2, -1)[u]) if u >= 3 or not isinstance(c, int) else 0)
                for i in range(2):
                    h = 2 * pair + i
                    mm = pe.matmul(s_tile(u)[:, i, :], ka[:, slot, h, kt * P:(kt + 1) * P], qa[:, slot, h, :], start=True, stop=True)
                mm.then_inc(qk_ready, 1)

            def values(c, step):
                g, kt = divmod(step, KT)
                pe.wait_ge(exp_done, 64 * c + 2 * step + 2)
                if kt == 0:
                    wait(pe, o_copied, 4 * c + g)
                for h in range(HG):
                    mm = pe.matmul(ps[32 * h:32 * h + VW, O_BANK, :], va[:, g % 2, kt, h, :], probs[:, step % 4, h, :],
                                   start=(kt == 0), stop=(kt == KT - 1))
                mm.then_inc(pv_done, 1)

            use = [0, 0]

            def mix(base):
                n = use[1]
                use[1] += 1
                wait(pe, mix_free, base + n)
                return ps[:, MIX_BANK, :]

            def o_transpose(base, c, g):
                bank = mix(base)
                pe.wait_ge(o_copied, 4 * c + g + 1)
                for i in range(TILES):
                    mm = pe.transpose(bank[:, i * P:(i + 1) * P], oT[:, g % 2, i * P:(i + 1) * P], ident[:])
                mm.then_inc(mix_ready, 1)

            def project(base, c, stage):
                bank = mix(base)
                if stage == 0:
                    pe.wait_ge(attn_ready, 4 * c + 4)
                    for i in range(TILES):
                        mm = pe.transpose(bank[:, i * P:(i + 1) * P], attn[:, i, :], ident[:])
                else:
                    for i in range(TILES):
                        mm = pe.matmul(bank[:, i * P:(i + 1) * P], attnT[:, i * P:(i + 1) * P], wp[:], start=True, stop=True)
                mm.then_inc(mix_ready, 1)

            def x_transpose(base, c):
                bank = mix(base)
                pe.wait_ge(x1_ready, c + 1)
                for i in range(TILES):
                    mm = pe.transpose(bank[:, i * P:(i + 1) * P], x1[:, i, :], ident[:])
                mm.then_inc(mix_ready, 1)

            def w_at(col0):
                return w_hi[:, col0:col0 + P], w_lo[:, col0:col0 + P]

            def up(base, c, i, passes):
                m, w = i // 2, (W1, W2)[i % 2]
                bank = mix(base)
                pe.wait_ge(xs_ready, c + 1)
                todo = [(a, x) for a in w_at(w + m * P)[:1 + (passes > 2)] for x in (x_hi[:], x_lo[:])]
                for j, (a, x) in enumerate(todo):
                    mm = pe.matmul(bank, a, x, start=(j == 0), stop=(j == len(todo) - 1))
                mm.then_inc(mix_ready, 1)

            def from_tiles(bank, c, layer, w_of, first, passes):
                for k in range(HM):
                    if first:
                        pe.wait_ge(g_ready, 12 * c + HM * layer + k + 1)
                    todo = [(w, x) for w in w_at(w_of(k))[:1 + (passes > 2)] for x in (g_hi[:, k, :], g_lo[:, k, :])]
                    for i, (w, x) in enumerate(todo):
                        mm = pe.matmul(bank, w, x, start=(k == 0 and i == 0), stop=(k == HM - 1 and i == len(todo) - 1))
                mm.then_inc(mix_ready, 1)

            def hidden(base, c, layer, m, passes):
                from_tiles(mix(base), c, layer, lambda k: (H1, H2)[layer] + k * HID + m * P, m == 0, passes)

            def down(base, c, passes):
                from_tiles(mix(base), c, 2, lambda k: W3 + k * P, True, passes)

            def y_transpose(base, c):
                bank = mix(base)
                pe.wait_ge(yT_ready, c + 1)
                for i in range(TILES):
                    mm = pe.transpose(bank[:, i * P:(i + 1) * P], yT[:, i * P:(i + 1) * P], ident[:])
                mm.then_inc(mix_ready, 1)

            def ffn_at(base, c, slot, passes):
                if slot == 3:
                    o_transpose(base, c, NG - 1)
                if slot == 5:
                    project(base, c, 0)
                if slot == 7:
                    project(base, c, 1)
                if slot == X_SLOT:
                    x_transpose(base, c)
                if slot in UP_SLOTS:
                    up(base, c, UP_SLOTS.index(slot), passes)
                for layer in range(2):
                    if slot in HIDDEN_SLOTS[layer]:
                        hidden(base, c, layer, HIDDEN_SLOTS[layer].index(slot), passes)
                if slot == DOWN_SLOT:
                    down(base, c, passes)
                if slot == Y_SLOT:
                    y_transpose(base, c)

            def chunk(c, passes):
                base = 0 if passes == 0 else MIX_CHUNK * (c - 1) + MIX_FIRST
                use[1] = 0
                for step in range(STEPS):
                    logits(c, step, 0)
                    if passes:
                        ffn_at(base, c - 1, 2 * step, passes)
                    logits(c, step, 1)
                    if step:
                        values(c, step - 1)
                    elif passes:
                        values(c - 1, STEPS - 1)
                    if passes:
                        ffn_at(base, c - 1, 2 * step + 1, passes)
                    if 2 * step + 1 in O_SLOTS:
                        o_transpose(base, c, O_SLOTS.index(2 * step + 1))
                    if not passes and 2 * step == FLAG_SLOT:
                        bank = mix(0)
                        pe.wait_ge(w_split, 1)
                        pe.matmul(bank[0:1, 0:1], ve[:, 0:1], ones_c[:], start=True, stop=True).then_inc(mix_ready, 1)

            def last_layer(done, bank0, w, rows, cols, passes, inputs):
                for k in range(rows):
                    inputs(k)
                    for m in range(cols):
                        if k == 0 and m == HM // 2 and w == H1:
                            pe.wait_ge(last_read, 2)
                        terms = [(a, x) for a in w_at(w + (k * HID if cols > 1 else k * P) + m * P)[:1 + (passes > 2)]
                                 for x in (g_hi[:, k, :], g_lo[:, k, :])]
                        for i, (a, x) in enumerate(terms):
                            mm = pe.matmul(ps[:, bank0 + m, :], a, x, start=(k == 0 and i == 0),
                                           stop=(k == rows - 1 and i == len(terms) - 1))
                        if k == rows - 1:
                            mm.then_inc(done, 1)

            def last_chunk(passes):
                c = NCH - 1

                def turned(step, bank0, src):
                    for hf in range(2):
                        pe.wait_ge(last_given, step + hf + 1)
                        for i in range(HT):
                            mm = pe.transpose(ps[:, bank0 + hf, i * P:(i + 1) * P], src(hf * HT + i), ident[:])
                        mm.then_inc(last_ready, 1)

                def keep_warm(count):
                    for _ in range(count):
                        pe.matmul(ps[:, MIX_BANK, :], warm[:, 0:P], warm[:], start=True, stop=True)

                values(c, STEPS - 1)
                turned(G_O, 0, lambda i: oT[:, (NG - 1) % 2, i * P:(i + 1) * P])
                turned(G_ATTN, 2, lambda i: attn[:, i, :])
                for hf in range(2):
                    pe.wait_ge(last_given, G_ATTN_T + hf + 1)
                    for i in range(HT):
                        mm = pe.matmul(ps[:, 4 + hf, i * P:(i + 1) * P], attnT[:, (hf * HT + i) * P:(hf * HT + i + 1) * P], wp[:],
                                       start=True, stop=True)
                    mm.then_inc(last_ready, 1)
                pe.wait_ge(mix_free, MIX_CHUNK * (NCH - 1) + MIX_FIRST)
                keep_warm(KEEP_WARM[0])
                turned(G_X, 0, lambda i: x1[:, i, :])
                keep_warm(KEEP_WARM[1])
                pe.wait_ge(last_given, G_SPLIT + 2)
                for m in range(HM):
                    for i, w in enumerate((W1, W2)):
                        terms = [(a, x) for a in w_at(w + m * P)[:1 + (passes > 2)] for x in (x_hi[:], x_lo[:])]
                        for j, (a, x) in enumerate(terms):
                            mm = pe.matmul(ps[:, 2 * m + i, :], a, x, start=(j == 0), stop=(j == len(terms) - 1))
                        mm.then_inc(last_up, 1)
                last_layer(last_hidden, 0, H1, HM, HM, passes, lambda k: pe.wait_ge(last_split, k + 1))
                last_layer(last_hidden, HM, H2, HM, HM, passes, lambda k: pe.wait_ge(last_split, HM + k + 1))
                last_layer(last_ready, 0, W3, HM, 1, passes, lambda k: pe.wait_ge(last_split, 2 * HM + k + 1))
                turned(G_Y, 1, lambda i: yT[:, i * P:(i + 1) * P])

            def later_chunks(passes):
                with pe.Fori(1, NCH) as c:
                    chunk(c, passes)
                    assert use[1] == MIX_CHUNK
                last_chunk(passes)

            pe.wait_ge(warm_set, 1)
            for _ in range(WARM):
                pe.matmul(ps[:, MIX_BANK, :], warm[:, 0:P], warm[:], start=True, stop=True)
            pe.wait_ge(in_w, 16)
            pe.wait_ge(in_small, 48)
            for t in range(NCH):
                prepare(t)
            pe.wait_ge(rot_done, NCH)
            pe.wait_ge(ln_done, NCH)
            pe.wait_ge(v_evac, NCH)
            pe.wait_ge(o_rows_set, 1)
            pe.wait_ge(in_res, 64)

            def row_maxima(n):
                pe.wait_ge(max_in, 16 * 3 * (n + 1))
                for u in range(MT):
                    h, t = divmod(u, KT)
                    if u >= 3:
                        pe.wait_ge(max_taken, MT * n + u - 2)
                    for i in range(2):
                        mm = pe.matmul(s_tile(u)[:, i, :], qa[:, t // TILES, h, (t % TILES) * P:(t % TILES + 1) * P],
                                       ka[:, 0, h, i * CH:(i + 1) * CH], start=True, stop=True)
                    mm.then_inc(max_logits, 1)
                pe.wait_ge(max_split, n + 2)
                pe.transpose(ps[0:PARTS * MT, MIX_BANK, 0:P], max_parts, ident[:]).then_inc(max_turned, 1)

            pe.wait_ge(bound_flag, 1)
            wide = pe.value_load(flags_i[0:1, 0:1], min_val=0, max_val=1)
            with pe.If(wide == 1):
                with pe.Fori(0, BATCH * NG) as n:
                    row_maxima(n)
                pe.wait_ge(max_rows, BATCH * NG)

            chunk(0, 0)
            pe.wait_ge(lo_flag, 1)
            low = pe.value_load(flags_i[0:1, 1:2], min_val=0, max_val=1)
            with pe.If(low == 0):
                later_chunks(2)
            with pe.If(low == 1):
                later_chunks(4)

        @block.scalar
        def _(act):
            act.preload_act_table_set("natural_log_exp_and_others")
            act.wait_ge(consts, 1)

            def part(i, t):
                if i == 0:
                    act.wait_ge(h_done, t + 1)
                    if t >= 2:
                        act.wait_ge(scr_out[t % 2], STORED)
                    nc.scalar.copy(parts[:, t % 2, 0, :], hn).then_inc(p1_done, 1)
                else:
                    act.wait_ge(res_done, t + 1)
                    nc.scalar.copy(parts[:, t % 2, 1, :], res).then_inc(p2_done, 1)

            for t in range(NCH):
                if t > 1:
                    part(0, t - 1)
                act.wait_ge(qk_proj, t + 1)
                wait(act, var_ready, t)
                nc.scalar.activation(sq, ps[:, 0:2, :].rearrange("p a q -> p (a q)"), ACT.Square).then_inc(sq_done, 1)
                if t:
                    part(int(t > 1), t - 1)
                act.wait_ge(var_ready, t + 1)
                wait(act, rinv_done, t)
                nc.scalar.activation(lnv, ps[:, 4:6, :].rearrange("p a q -> p (a q)"), ACT.Ln, bias=eps_c[:]).then_inc(ln_done, 1)
                act.wait_ge(ln_done, t + 1)
                wait(act, h_done, t)
                nc.scalar.activation(rinv, lnv, ACT.Exp, scale=-0.5).then_inc(rinv_done, 1)
                if t == 1:
                    part(1, 0)
                act.wait_ge(v_proj, t + 1)
                if t == 0:
                    act.wait_ge(v_ones, 1)
                for i in range(TILES):
                    kt = (t % 2) * TILES + i
                    ins = nc.scalar.copy(v_all[:, t // 2, :, kt, :, 0:HD],
                                         ps[:, 6 + t % 2, i * P:(i + 1) * P].rearrange("p (g h d) -> p g h d", g=NG, h=HG))
                ins.then_inc(v_evac, 1)
            act.preload_act_table_set("exp_and_others")
            part(0, NCH - 1)
            part(1, NCH - 1)

            def exps(c, step):
                for pair in range(2):
                    u = 2 * step + pair
                    act.wait_ge(qk_ready, 64 * c + u + 1)
                    if pair == 0:
                        wait(act, pv_done, 32 * c + step - 3)
                    nc.scalar.activation(probs[:, step % 4, 2 * pair:2 * pair + 2, :], s_tile(u), ACT.Exp).then_inc(exp_done, 1)

            def gate(c, m):
                act.wait_ge(pre_ready, 8 * c + m + 1)
                nc.scalar.activation(act_o[:, m * CH:(m + 1) * CH], pre_a[:, m * CH:(m + 1) * CH], ACT.Tanh, scale=0.5).then_inc(act_done, 1)

            def gelu(c, layer):
                for i, tiles in enumerate(GELU_TILES):
                    act.wait_ge(pre_ready, 8 * c + HM + 2 * layer + i + 1)
                    cols = slice(tiles[0] * CH, (tiles[-1] + 1) * CH)
                    nc.scalar.activation(act_o[:, cols], pre_a[:, cols], ACT.Gelu).then_inc(act_done, 1)

            for step in range(STEPS):
                if step == 2:
                    act.wait_ge(p3_done, NCH)
                exps(0, step)
            with act.Fori(1, NCH) as c:
                for step in range(STEPS):
                    exps(c, step)
                    if step in GATE_STEPS:
                        gate(c - 1, GATE_STEPS.index(step))
                    if step in GELU_STEPS:
                        gelu(c - 1, GELU_STEPS.index(step))

            act.preload_act_table(ACT.Silu)
            for m in range(HM):
                act.wait_ge(last_up, 2 * m + 1)
                nc.scalar.activation(act_o[:, m * CH:(m + 1) * CH], ps[:, 2 * m, :], ACT.Silu, scale=col[:, C_S1 + m:C_S1 + m + 1]).then_inc(last_act, 1)
            act.preload_act_table(ACT.Gelu)
            for layer in range(2):
                for m in range(HM):
                    act.wait_ge(last_hidden, HM * layer + m + 1)
                    act.wait_ge(last_split, HM * layer + m + 1)
                    nc.scalar.activation(act_o[:, m * CH:(m + 1) * CH], ps[:, HM * layer + m, :], ACT.Gelu,
                                         scale=col[:, (C_H1, C_H2)[layer] + m:(C_H1, C_H2)[layer] + m + 1]).then_inc(last_act, 1)
            act.wait_ge(last_act, 3 * HM)
            for m in range(HM // 2, HM):
                nc.scalar.copy(g_hi[:, m, :], act_o[:, m * CH:(m + 1) * CH]).then_inc(last_high, 1)

        @block.vector
        def _(dve):
            links = [0]

            def link(ins, base):
                links[0] += 1
                ins.then_inc(chain, 1)
                dve.wait_ge(chain, base + links[0])

            nc.vector.memset(warm[:], 0.0).then_inc(warm_set, 1)
            nc.vector.memset(eps_c[:], EPS_RMS)
            nc.vector.memset(ones_c[:], 1.0).then_inc(consts, 1)
            dve.wait_ge(in_small, 48)
            for i in range(2):
                ins = nc.vector.tensor_reduce(flags[:, i:i + 1], srow[:, i * HD:(i + 1) * HD], AX.X, ALU.max, apply_absolute_value=True)
            link(ins, 0)
            link(nc.vector.tensor_scalar(flags[:, 2:3], flags[:, 0:1], flags[:, 1:2], HD ** 0.5, ALU.mult, ALU.mult), 0)
            link(nc.vector.tensor_scalar(flags[:, 3:4], flags[:, 2:3], LOGIT_BOUND, None, ALU.is_gt), 0)
            nc.vector.tensor_copy(flags_i[:, 0:1], flags[:, 3:4]).then_inc(bound_flag, 1)
            link(nc.vector.tensor_scalar(col[:, C_Q:C_QS + 1], col[:, C_Q:C_QS + 1], HD ** -0.5, None, ALU.mult), 0)
            nc.vector.tensor_scalar(col[:, C_S2H:C_S2H + HM], col[:, C_S2:C_S2 + HM], 0.5, None, ALU.mult)
            dve.wait_ge(in_rope, 32)

            def residue(t):
                dve.wait_ge(p1_done, t + 1)
                dve.wait_ge(h_done, t + 1)
                wait(dve, p3_done, t)
                nc.vector.tensor_tensor(res, hn, parts[:, t % 2, 0, :], ALU.subtract).then_inc(res_done, 1)

            for t in range(NCH):
                half = (t % 2) * CH
                dve.wait_ge(qk_proj, t + 1)
                for i, c_, table, dst in ((2, C_QS, sinT, rot_b), (3, C_KS, sinT, rot_b), (0, C_Q, cosT, rot_a), (1, C_K, cosT, rot_a)):
                    if i == 0:
                        if t > 1:
                            residue(t - 1)
                            dve.wait_ge(res_done, t)
                        dve.wait_ge(sq_done, t + 1)
                        wait(dve, h_done, t)
                    ins = nc.vector.scalar_tensor_tensor(
                        out=dst[:, (i % 2) * CH:(i % 2 + 1) * CH], in0=ps[:, i, :], scalar=col[:, c_:c_ + 1],
                        in1=table[:, half:half + CH], op0=ALU.mult, op1=ALU.mult)
                ins.then_inc(rot_done, 1)
                dve.wait_ge(rot_done, t + 1)
                link(nc.vector.tensor_tensor(rot_a, rot_a, rot_b, ALU.add), 0)
                if t == 1:
                    residue(0)
                    dve.wait_ge(res_done, 1)
                dve.wait_ge(rinv_done, t + 1)
                nc.vector.tensor_tensor(hn, rot_a, rinv, ALU.mult).then_inc(h_done, 1)
            dve.wait_ge(v_evac, NCH - 1)
            nc.vector.memset(ps[:, O_BANK, :], 0.0).then_inc(o_rows_set, 1)
            residue(NCH - 1)

            use = [0]

            def mixed(base):
                n = use[0]
                use[0] += 1
                dve.wait_ge(mix_ready, base + n + 1)
                return n

            mix_bank = ps[:, MIX_BANK, :]

            def copy_o(c, g):
                dve.wait_ge(pv_done, KT * (4 * c + g + 1))
                nc.vector.tensor_copy(oT[:, g % 2, :], ps[:, O_BANK, :]).then_inc(o_copied, 1)

            def normalise(base, cb, g):
                n = mixed(base)
                bank = mix_bank.rearrange("p (t h r) -> p t h r", t=TILES, h=HG)
                link(nc.vector.reciprocal(rden[:], bank[:, :, :, HD]), cb)
                dst = attn[:, :, g * 32:(g + 1) * 32].rearrange("p t (h d) -> p t h d", h=HG)
                nc.vector.tensor_tensor(dst, bank[:, :, :, 0:HD], rden[:, :, :, None].to_broadcast([P, TILES, HG, HD]),
                                        ALU.mult).then_inc(mix_free, 1)
                dve.wait_ge(mix_free, base + n + 1)
                dve.nop().then_inc(attn_ready, 1)

            def layer_norm(cb, src):
                for i in range(TILES):
                    ins = nc.vector.bn_stats(stats[:, i, :], src[:, i, :])
                link(ins, cb)
                nc.vector.memset(ve[:], 0.0)
                for i in range(TILES):
                    ins = nc.vector.bn_aggr(mv[:, i, :], stats[:, i, :])
                link(ins, cb)
                nc.vector.tensor_scalar(ve[:], mv[:, :, 1], EPS_LN, None, ALU.add).then_inc(var1, 1)

            def scale_rows_of(n, src, dst):
                dve.wait_ge(rstd, n)
                for i in range(TILES):
                    ins = nc.vector.tensor_scalar(dst[:, i, :], src[:, i, :], mv[:, i, 0:1], rs[:, i:i + 1],
                                                  ALU.subtract, ALU.mult)
                return ins

            def split(cb, src, hi, lo):
                link(nc.vector.tensor_copy(hi, src), cb)
                return nc.vector.tensor_tensor(lo, src, hi.bitcast(F32), ALU.subtract)

            def residual(base, cb, c):
                n = mixed(base)
                xr = xb[:].rearrange("p t c -> p (t c)")[:, bass.ds(c * CH, CH)]
                nc.vector.tensor_tensor(r1[:].rearrange("p t c -> p (t c)"), mix_bank, xr, ALU.add).then_inc(mix_free, 1)
                dve.wait_ge(mix_free, base + n + 1)
                layer_norm(cb, r1)
                scale_rows_of(2 * c + 1, r1, x1).then_inc(x1_ready, 1)

            def split_x(base, cb):
                n = mixed(base)
                split(cb, mix_bank, x_hi[:], x_lo[:]).then_inc(mix_free, 1)
                dve.wait_ge(mix_free, base + n + 1)
                dve.nop().then_inc(xs_ready, 1)

            def copy_attention(base):
                mixed(base)
                nc.vector.tensor_copy(attnT, mix_bank).then_inc(mix_free, 1)

            def pre_activation(base, m, c0, signal, gated=False):
                n = mixed(base)
                a, b = (v[:, m * CH:(m + 1) * CH] for v in (pre_a, pre_b))
                if gated:
                    ins = nc.vector.scalar_tensor_tensor(out=b, in0=mix_bank, scalar=col[:, c0 + m:c0 + m + 1], in1=a,
                                                         op0=ALU.mult, op1=ALU.mult)
                else:
                    ins = nc.vector.tensor_scalar(a, mix_bank, col[:, c0 + m:c0 + m + 1], None, ALU.mult)
                ins.then_inc(mix_free, 1)
                if signal:
                    dve.wait_ge(mix_free, base + n + 1)
                    dve.nop().then_inc(pre_ready, 1)

            def split_tile(cb, m):
                cols_m = act_o[:, m * CH:(m + 1) * CH]
                return split(cb, cols_m, g_hi[:, m, :], g_lo[:, m, :])

            def gate(cb, c, m):
                a, b = (v[:, m * CH:(m + 1) * CH] for v in (act_o, pre_b))
                dve.wait_ge(act_done, 8 * c + m + 1)
                link(nc.vector.scalar_tensor_tensor(out=a, in0=a, scalar=1.0, in1=b, op0=ALU.add, op1=ALU.mult), cb)
                split_tile(cb, m).then_inc(g_ready, 1)

            def gelu_split(cb, c, layer):
                for i, tiles in enumerate(GELU_TILES):
                    dve.wait_ge(act_done, 8 * c + HM + 2 * layer + i + 1)
                    for m in tiles:
                        split_tile(cb, m).then_inc(g_ready, 1)

            def scale_y(base, c):
                n = mixed(base)
                nc.vector.tensor_scalar(yT, mix_bank, col[:, C_W3:C_W3 + 1], None, ALU.mult).then_inc(mix_free, 1)
                dve.wait_ge(mix_free, base + n + 1)
                dve.nop().then_inc(yT_ready, 1)

            def finish(base, cb, c):
                n = mixed(base)
                nc.vector.tensor_tensor(r1[:].rearrange("p t c -> p (t c)"), mix_bank,
                                        x1.rearrange("p t c -> p (t c)"), ALU.add).then_inc(mix_free, 1)
                dve.wait_ge(mix_free, base + n + 1)
                layer_norm(cb, r1)
                dve.wait_ge(yo_free, c + 1)
                scale_rows_of(2 * c + 2, r1, yo).then_inc(y_ready, 1)

            def ffn_at(base, cb, c, slot):
                if slot == 3:
                    normalise(base, cb, NG - 1)
                if slot == 5:
                    copy_attention(base)
                if slot == 7:
                    residual(base, cb, c)
                if slot == X_SLOT:
                    split_x(base, cb)
                if slot in UP_SLOTS:
                    i = UP_SLOTS.index(slot)
                    pre_activation(base, i // 2, (C_S1, C_S2H)[i % 2], i % 2 == 1, gated=i % 2 == 1)
                if slot in GATE_SLOTS:
                    gate(cb, c, GATE_SLOTS.index(slot))
                for layer in range(2):
                    if slot in HIDDEN_SLOTS[layer]:
                        m = HIDDEN_SLOTS[layer].index(slot)
                        pre_activation(base, m, (C_H1, C_H2)[layer], m >= HM - 2)
                    if slot == SPLIT_SLOTS[layer]:
                        gelu_split(cb, c, layer)
                if slot == DOWN_SLOT:
                    scale_y(base, c)
                if slot == Y_SLOT:
                    finish(base, cb, c)

            def chunk(c, base, cb, with_ffn):
                for step in range(STEPS):
                    g, kt = divmod(step, KT)
                    if with_ffn:
                        ffn_at(base, cb, c - 1, 2 * step)
                    if kt == 0 and g:
                        copy_o(c, g - 1)
                    if kt == 0 and g == 0 and with_ffn:
                        copy_o(c - 1, NG - 1)
                    if with_ffn:
                        ffn_at(base, cb, c - 1, 2 * step + 1)
                    if 2 * step + 1 in O_SLOTS:
                        normalise(base, cb, O_SLOTS.index(2 * step + 1))
                    if not with_ffn and 2 * step == FLAG_SLOT:
                        mixed(0)
                        link(nc.vector.tensor_scalar(flags[:, 0:1], mix_bank[0:1, 0:1], 0.0, None, ALU.not_equal), 0)
                        nc.vector.tensor_copy(flags_i[:, 1:2], flags[:, 0:1]).then_inc(lo_flag, 1)
                        dve.nop().then_inc(mix_free, 1)

            def max_link(ins, n, k):
                ins.then_inc(max_chain, 1)
                dve.wait_ge(max_chain, 5 * n + k)

            def row_maxima(n):
                for u in range(MT):
                    dve.wait_ge(max_logits, MT * n + u + 1)
                    ins = nc.vector.tensor_reduce(neg_max[:, u:u + 1], s_tile(u).rearrange("p a q -> p (a q)"), AX.X, ALU.max, negate=True)
                    ins.then_inc(max_taken, 1)
                dve.wait_ge(max_taken, MT * (n + 1))
                src = neg_max
                for i in range(PARTS):
                    max_link(nc.vector.tensor_copy(part16, src), n, 2 * i + 1)
                    if i < PARTS - 1:
                        nc.vector.tensor_copy(max_parts[:, i * MT:(i + 1) * MT], part16)
                        max_link(nc.vector.tensor_tensor(max_res, src, part16, ALU.subtract), n, 2 * i + 2)
                    else:
                        nc.vector.tensor_copy(max_parts[:, i * MT:(i + 1) * MT], part16).then_inc(max_split, 1)
                    src = max_res
                dve.wait_ge(max_turned, n + 1)
                nc.vector.tensor_copy(max_row, ps[0:PARTS * MT, MIX_BANK, 0:P]).then_inc(max_rows, 1)
                dve.wait_ge(max_stored, 16 * PARTS * (n + 1))

            wide = dve.value_load(flags_i[0:1, 0:1], min_val=0, max_val=1)
            with dve.If(wide == 1):
                dve.nop().then_inc(max_split, 1)
                with dve.Fori(0, BATCH * NG) as n:
                    row_maxima(n)

            dve.wait_ge(in_ffn, 80)
            link(nc.vector.tensor_copy(w_hi[:], w_raw), 0)
            link(nc.vector.tensor_tensor(w_lo[:], w_raw, w_hi[:].bitcast(F32), ALU.subtract), 0)
            nc.vector.tensor_reduce(ve[:, 0:1], w_lo[:].bitcast(F32), AX.X, ALU.max, apply_absolute_value=True).then_inc(w_split, 1)
            chunk(0, 0, 0, False)
            dve.wait_ge(res_add, 1)
            start = links[0]
            with dve.Fori(1, NCH) as c:
                use[0], links[0] = 0, 0
                chunk(c, MIX_CHUNK * (c - 1) + MIX_FIRST, CHAIN_CHUNK * (c - 1) + start, True)
                assert use[0] == MIX_CHUNK and links[0] == CHAIN_CHUNK, links[0]

            use[0], links[0] = 0, 0
            c, base, cb = NCH - 1, MIX_CHUNK * (NCH - 1) + MIX_FIRST, CHAIN_CHUNK * (NCH - 1) + start
            half_of = lambda v, hf: v[:, hf * HC:(hf + 1) * HC]

            def last_norm(hf, a, b):
                tiles = range(hf * HT, (hf + 1) * HT)
                link(nc.vector.tensor_tensor(half_of(r1[:].rearrange("p t c -> p (t c)"), hf), a, b, ALU.add), cb)
                for i in tiles:
                    ins = nc.vector.bn_stats(stats[:, i, :], r1[:, i, :])
                link(ins, cb)
                for i in tiles:
                    ins = nc.vector.bn_aggr(mv[:, i, :], stats[:, i, :])
                link(ins, cb)
                nc.vector.tensor_scalar(ve[:, tiles[0]:tiles[-1] + 1], mv[:, tiles[0]:tiles[-1] + 1, 1], EPS_LN, None, ALU.add).then_inc(last_var, 1)

            def last_scaled(n, hf, dst):
                dve.wait_ge(last_rstd, n + 1)
                for i in range(hf * HT, (hf + 1) * HT):
                    ins = nc.vector.tensor_scalar(dst[:, i, :], r1[:, i, :], mv[:, i, 0:1], rs[:, i:i + 1], ALU.subtract, ALU.mult)
                return ins

            dve.wait_ge(pv_done, KT * NG * NCH)
            for hf in range(2):
                nc.vector.tensor_copy(half_of(oT[:, (NG - 1) % 2, :], hf), half_of(ps[:, O_BANK, :], hf)).then_inc(last_given, 1)
            for hf in range(2):
                dve.wait_ge(last_ready, R_O + hf + 1)
                bank = ps[:, hf, 0:HC].rearrange("p (t h r) -> p t h r", t=HT, h=HG)
                tiles = slice(hf * HT, (hf + 1) * HT)
                link(nc.vector.reciprocal(rden[:, tiles], bank[:, :, :, HD]), cb)
                nc.vector.tensor_tensor(attn[:, tiles, (NG - 1) * 32:NG * 32].rearrange("p t (h d) -> p t h d", h=HG), bank[:, :, :, 0:HD],
                                        rden[:, tiles, :, None].to_broadcast([P, HT, HG, HD]), ALU.mult).then_inc(last_given, 1)
            for hf in range(2):
                dve.wait_ge(last_ready, R_ATTN + hf + 1)
                nc.vector.tensor_copy(half_of(attnT, hf), ps[:, 2 + hf, 0:HC]).then_inc(last_given, 1)
            xr = xb[:, c * TILES:(c + 1) * TILES, :].rearrange("p t c -> p (t c)")
            for hf in range(2):
                dve.wait_ge(last_ready, R_PROJ + hf + 1)
                last_norm(hf, ps[:, 4 + hf, 0:HC], half_of(xr, hf))
            for hf in range(2):
                last_scaled(hf, hf, x1).then_inc(last_given, 1)
            for hf in range(2):
                dve.wait_ge(last_ready, R_X + hf + 1)
                split(cb, ps[:, hf, 0:HC], half_of(x_hi, hf), half_of(x_lo, hf)).then_inc(last_given, 1)
            for m in range(HM):
                a = act_o[:, m * CH:(m + 1) * CH]
                dve.wait_ge(last_act, m + 1)
                dve.wait_ge(last_up, 2 * m + 2)
                nc.vector.scalar_tensor_tensor(out=a, in0=ps[:, 2 * m + 1, :], scalar=col[:, C_S2 + m:C_S2 + m + 1],
                                               in1=a, op0=ALU.mult, op1=ALU.mult).then_inc(last_read, 1)
                dve.wait_ge(last_read, m + 1)
                split_tile(cb, m).then_inc(last_split, 1)
            for layer in range(2):
                for m in range(HM):
                    dve.wait_ge(last_act, HM * (layer + 1) + m + 1)
                    if layer == 1 and m >= HM // 2:
                        dve.wait_ge(last_high, m - HM // 2 + 1)
                        tile_m = act_o[:, m * CH:(m + 1) * CH]
                        nc.vector.tensor_tensor(g_lo[:, m, :], tile_m, g_hi[:, m, :].bitcast(F32), ALU.subtract).then_inc(last_split, 1)
                    else:
                        split_tile(cb, m).then_inc(last_split, 1)
            dve.wait_ge(last_ready, R_DOWN + 1)
            for hf in range(2):
                nc.vector.tensor_scalar(half_of(yT, hf), half_of(ps[:, 0, :], hf), col[:, C_W3:C_W3 + 1], None, ALU.mult).then_inc(last_given, 1)
            for hf in range(2):
                dve.wait_ge(last_ready, R_Y + hf + 1)
                last_norm(hf, ps[:, 1 + hf, 0:HC], half_of(x1.rearrange("p t c -> p (t c)"), hf))
            dve.wait_ge(yo_free, c + 1)
            for hf in range(2):
                last_scaled(2 + hf, hf, yo).then_inc(last_y, 1)


def kernel(**inputs):
    import concourse.bacc as bacc
    from concourse.bass_utils import run_bass_kernel_spmd

    a = {k.split("_", 1)[1]: np.ascontiguousarray(v) for k, v in inputs.items()}
    x = a["attn_x"].reshape(TOK, DIM)
    swap = (np.arange(DIM) // HD) * HD + (np.arange(DIM) + HD // 2) % HD
    w = a["attn_w_qkv"]
    w_q, w_k, w_v = w[:, :DIM], w[:, DIM:2 * DIM], w[:, 2 * DIM:]
    d_of = np.arange(DIM) % HD
    q_s, k_s = a["attn_q_scale"][d_of], a["attn_k_scale"][d_of]
    by_tile = lambda s: s.reshape(HM, P).T
    half = HD // 2
    freqs = (np.float32(1.0) / np.float32(1250) ** (np.arange(half, dtype=np.float32) / np.float32(half))).astype(np.float32)
    angle = np.outer(np.arange(SEQ, dtype=np.float32), freqs).astype(np.float32)[:, d_of % half].T
    sign = np.where(d_of < half, -1.0, 1.0).astype(np.float32)[:, None]
    same_head = np.arange(P)[:, None] // HD == np.arange(P)[None, :] // HD
    arrays = {
        "x_t": x.T, "x_n": x,
        "w_qkv": np.concatenate([w_q, w_k, w_q[:, swap], w_k[:, swap], w_v], axis=1),
        "cols": np.concatenate([by_tile(a["ffn_w1_s"]), by_tile(a["ffn_w2_s"]), by_tile(a["ffn_h1_s"]), by_tile(a["ffn_h2_s"]),
                                a["ffn_w3_s"][:, None], q_s[:, None], q_s[swap][:, None], k_s[:, None], k_s[swap][:, None]], axis=1),
        "scale_rows": np.concatenate([a["attn_q_scale"], a["attn_k_scale"]])[None, :],
        "bias": np.broadcast_to(a["attn_b_proj"][None, :], (P, DIM)),
        "w_proj": a["attn_w_proj"],
        "w1": a["ffn_w1_w"].T, "w2": a["ffn_w2_w"].T, "h1": a["ffn_h1_w"].T, "h2": a["ffn_h2_w"].T, "w3": a["ffn_w3_w"].T,
        "cosines": np.cos(angle).astype(np.float32), "sines": (np.sin(angle) * sign).astype(np.float32),
        "means": (same_head / HD).astype(np.float32), "eye": np.eye(P, dtype=np.float32),
    }
    nc = bacc.Bacc("TRN2", target_bir_lowering=False, num_devices=1)
    sent, args = {}, []
    for name, v in arrays.items():
        v = np.ascontiguousarray(v)
        sent[f"in_{name}"] = v
        args.append(nc.dram_tensor(f"in_{name}", v.shape, mybir.dt.from_np(v.dtype), kind="ExternalInput").ap())
    out = nc.dram_tensor("out_y", (TOK, DIM), F32, kind="ExternalOutput").ap()
    build(nc, *args, out)
    r = run_bass_kernel_spmd(nc, [sent], core_ids=[0])
    return r.results[0]["out_y"].reshape(BATCH, SEQ, DIM)
```
